# Optimizing a Trainium2 kernel written in Bass

```python
import numpy as np
import jax
import jax.numpy as jnp

def _softmax(x, axis=-1):
    return jax.nn.softmax(x, axis=axis)

def _gelu(x):
    return jax.nn.gelu(x, approximate=True)

def _silu(x):
    return jax.nn.silu(x)

def _sigmoid(x):
    return jax.nn.sigmoid(x)

def _layernorm(x, axis=-1, eps=1e-05):
    m = jnp.mean(x, axis=axis, keepdims=True)
    v = jnp.var(x, axis=axis, keepdims=True)
    return (x - m) / jnp.sqrt(v + eps)

def _scatter_add(tgt, idx, src, axis=0):
    return tgt.at[idx].add(src)

def _segment_sum(src, seg, n):
    return jax.ops.segment_sum(src, seg, n)
kernel_name = 'mk_gnn_preln_d2_gnn_r8_5d7da8'

def setup_inputs(seed: int=0):
    np.random.seed(seed)
    _w = jnp.asarray

    def _rec_inputs():
        import jax
        import jax.numpy as jnp
        _gk = jax.random.key(seed)
        x = -0.0002117 + 1 * jax.random.normal(jax.random.fold_in(_gk, 1), (6250, 512), jnp.float32)
        src = jax.random.randint(jax.random.fold_in(_gk, 2), (100000,), 0, 6250, jnp.int32)
        dst = jnp.minimum((6250 * jax.random.uniform(jax.random.fold_in(_gk, 3), (100000,)) ** 2.0).astype(jnp.int32), 49999)
        _o = jnp.argsort(dst, stable=True)
        src = src[_o]
        dst = dst[_o]
        edge_attr_4 = 0.00171547 + 0.999346 * jax.random.normal(jax.random.fold_in(_gk, 11), (100000, 4), jnp.float32)
        edge_attr_8 = 0.000126197 + 0.999763 * jax.random.normal(jax.random.fold_in(_gk, 12), (100000, 8), jnp.float32)
        return (x, src, dst, edge_attr_4, edge_attr_8)
    x, src, dst, edge_attr_4, edge_attr_8 = _rec_inputs()

    def _L0_gnn_setup():
        import jax, jax.numpy as jnp
        import numpy as np
        N = 6250
        E = 50000
        D_IN = 512
        D_H = 512
        D_OUT = 512
        LN_EPS = 1e-05

        def _layer_norm(x, g, b):
            mu = jnp.mean(x, axis=-1, keepdims=True)
            var = jnp.mean(jnp.square(x - mu), axis=-1, keepdims=True)
            return (x - mu) * jax.lax.rsqrt(var + LN_EPS) * g + b

        def _gcn_conv(x, row, col, W, bias):
            xw = x @ W
            ew = jnp.ones(row.shape[0], x.dtype)
            deg = jax.ops.segment_sum(ew, col, num_segments=N)
            dinv = jnp.where(deg > 0, jax.lax.rsqrt(deg), 0.0)
            norm = dinv[row] * dinv[col]
            out = jax.ops.segment_sum(norm[:, None] * xw[row], col, num_segments=N)
            return out + bias
        key = jax.random.key(seed)
        ks = jax.random.split(key, 16)
        s = 0.02
        return {'x': jax.random.normal(ks[0], (N, D_IN), jnp.float32), 'edge_index': jax.random.randint(ks[1], (2, E), 0, N, jnp.int64 if jax.config.jax_enable_x64 else jnp.int32), 'W0': jax.random.normal(ks[2], (D_IN, D_H), jnp.float32) * s, 'b0': jnp.zeros((D_H,), jnp.float32), 'lw0': jax.random.normal(ks[3], (D_H, D_IN), jnp.float32) * s, 'lb0': jnp.zeros((D_H,), jnp.float32), 'g0': jnp.ones((D_IN,), jnp.float32), 'be0': jnp.zeros((D_IN,), jnp.float32), 'W1': jax.random.normal(ks[4], (D_H, D_H), jnp.float32) * s, 'b1': jnp.zeros((D_H,), jnp.float32), 'lw1': jax.random.normal(ks[5], (D_H, D_H), jnp.float32) * s, 'lb1': jnp.zeros((D_H,), jnp.float32), 'g1': jnp.ones((D_H,), jnp.float32), 'be1': jnp.zeros((D_H,), jnp.float32), 'pw': jax.random.normal(ks[6], (D_OUT, D_H), jnp.float32) * s, 'pb': jnp.zeros((D_OUT,), jnp.float32)}
    _L0_gnn_all = _L0_gnn_setup()
    _L0_gnn_in = {k: v for k, v in _L0_gnn_all.items() if k in ('W0', 'b0', 'lw0', 'lb0', 'g0', 'be0', 'W1', 'b1', 'lw1', 'lb1', 'g1', 'be1', 'pw', 'pb')}
    del _L0_gnn_all

    def _L1_gnn_setup():
        import jax, jax.numpy as jnp
        import numpy as np
        MUL = 128
        N_NODES = 1250
        N_EDGES = 20000
        R_BASIS = 8
        HIDDEN = 64
        W_NUMEL = 4 * MUL
        SQRT3 = 3.0 ** 0.5
        SILU_2MOM = 1.679177
        AVG_NUM_NEIGHBORS = 10.0

        def _lin_irreps(x0, x1, W0, W1):
            y0 = x0 @ W0 / jnp.sqrt(jnp.float32(W0.shape[0]))
            y1 = jnp.einsum('num,uv->nvm', x1, W1) / jnp.sqrt(jnp.float32(W1.shape[0]))
            return (y0, y1)

        def _forward(node_feats, edge_attrs, edge_feats, edge_index, W_up0, W_up1, W_mlp1, W_mlp2, W_mlp3, W_mlp4, W_out0, W_out1):
            num_nodes = node_feats.shape[0]
            sender, receiver = (edge_index[0], edge_index[1])
            x0 = node_feats[:, :MUL]
            x1 = node_feats[:, MUL:].reshape(num_nodes, MUL, 3)
            x0, x1 = _lin_irreps(x0, x1, W_up0, W_up1)
            h = edge_feats
            for W in (W_mlp1, W_mlp2, W_mlp3):
                h = SILU_2MOM * jax.nn.silu(h @ W / jnp.sqrt(jnp.float32(W.shape[0])))
            tpw = h @ W_mlp4 / jnp.sqrt(jnp.float32(W_mlp4.shape[0]))
            w1, w2, w3, w4 = jnp.split(tpw, 4, axis=-1)
            s0 = x0[sender]
            s1 = x1[sender]
            y0 = edge_attrs[:, 0:1]
            y1 = edge_attrs[:, 1:4]
            p1 = w1 * s0 * y0
            p2 = (w2 * s0)[:, :, None] * y1[:, None, :]
            p3 = w3[:, :, None] * s1 * y0[:, None, :]
            p4 = w4 * jnp.einsum('eum,em->eu', s1, y1) / SQRT3
            m0 = jnp.concatenate([p1, p4], axis=-1)
            m1 = jnp.concatenate([p2, p3], axis=1)
            msg0 = jax.ops.segment_sum(m0, receiver, num_segments=num_nodes)
            msg1 = jax.ops.segment_sum(m1, receiver, num_segments=num_nodes)
            o0, o1 = _lin_irreps(msg0, msg1, W_out0, W_out1)
            out = jnp.concatenate([o0, o1.reshape(num_nodes, 3 * MUL)], axis=-1)
            return out / AVG_NUM_NEIGHBORS
        key = jax.random.key(seed)
        ks = jax.random.split(key, 12)
        rn = lambda k, s: jax.random.normal(k, s, dtype=jnp.float32)
        return {'node_feats': rn(ks[0], (N_NODES, 4 * MUL)), 'edge_attrs': rn(ks[1], (N_EDGES, 4)), 'edge_feats': rn(ks[2], (N_EDGES, R_BASIS)), 'edge_index': jax.random.randint(ks[3], (2, N_EDGES), 0, N_NODES), 'W_up0': rn(ks[4], (MUL, MUL)), 'W_up1': rn(ks[5], (MUL, MUL)), 'W_mlp1': rn(ks[6], (R_BASIS, HIDDEN)), 'W_mlp2': rn(ks[7], (HIDDEN, HIDDEN)), 'W_mlp3': rn(ks[8], (HIDDEN, HIDDEN)), 'W_mlp4': rn(ks[9], (HIDDEN, W_NUMEL)), 'W_out0': rn(ks[10], (2 * MUL, MUL)), 'W_out1': rn(ks[11], (2 * MUL, MUL))}
    _L1_gnn_all = _L1_gnn_setup()
    _L1_gnn_in = {k: v for k, v in _L1_gnn_all.items() if k in ('W_up0', 'W_up1', 'W_mlp1', 'W_mlp2', 'W_mlp3', 'W_mlp4', 'W_out0', 'W_out1')}
    del _L1_gnn_all
    return {'x': x, 'src': src, 'dst': dst, 'edge_attr_4': edge_attr_4, 'edge_attr_8': edge_attr_8, 'L0_gnn_W0': _L0_gnn_in['W0'], 'L0_gnn_b0': _L0_gnn_in['b0'], 'L0_gnn_lw0': _L0_gnn_in['lw0'], 'L0_gnn_lb0': _L0_gnn_in['lb0'], 'L0_gnn_g0': _L0_gnn_in['g0'], 'L0_gnn_be0': _L0_gnn_in['be0'], 'L0_gnn_W1': _L0_gnn_in['W1'], 'L0_gnn_b1': _L0_gnn_in['b1'], 'L0_gnn_lw1': _L0_gnn_in['lw1'], 'L0_gnn_lb1': _L0_gnn_in['lb1'], 'L0_gnn_g1': _L0_gnn_in['g1'], 'L0_gnn_be1': _L0_gnn_in['be1'], 'L0_gnn_pw': _L0_gnn_in['pw'], 'L0_gnn_pb': _L0_gnn_in['pb'], 'L1_gnn_W_up0': _L1_gnn_in['W_up0'], 'L1_gnn_W_up1': _L1_gnn_in['W_up1'], 'L1_gnn_W_mlp1': _L1_gnn_in['W_mlp1'], 'L1_gnn_W_mlp2': _L1_gnn_in['W_mlp2'], 'L1_gnn_W_mlp3': _L1_gnn_in['W_mlp3'], 'L1_gnn_W_mlp4': _L1_gnn_in['W_mlp4'], 'L1_gnn_W_out0': _L1_gnn_in['W_out0'], 'L1_gnn_W_out1': _L1_gnn_in['W_out1']}

def reference(x, src, dst, edge_attr_4, edge_attr_8, L0_gnn_W0, L0_gnn_b0, L0_gnn_lw0, L0_gnn_lb0, L0_gnn_g0, L0_gnn_be0, L0_gnn_W1, L0_gnn_b1, L0_gnn_lw1, L0_gnn_lb1, L0_gnn_g1, L0_gnn_be1, L0_gnn_pw, L0_gnn_pb, L1_gnn_W_up0, L1_gnn_W_up1, L1_gnn_W_mlp1, L1_gnn_W_mlp2, L1_gnn_W_mlp3, L1_gnn_W_mlp4, L1_gnn_W_out0, L1_gnn_W_out1):
    import jax
    import jax.numpy as jnp

    def _L0_gnn_ref(x, edge_index, W0, b0, lw0, lb0, g0, be0, W1, b1, lw1, lb1, g1, be1, pw, pb):
        import jax, jax.numpy as jnp
        import numpy as np
        N = 6250
        E = 50000
        D_IN = 512
        D_H = 512
        D_OUT = 512
        LN_EPS = 1e-05

        def _layer_norm(x, g, b):
            mu = jnp.mean(x, axis=-1, keepdims=True)
            var = jnp.mean(jnp.square(x - mu), axis=-1, keepdims=True)
            return (x - mu) * jax.lax.rsqrt(var + LN_EPS) * g + b

        def _gcn_conv(x, row, col, W, bias):
            xw = x @ W
            ew = jnp.ones(row.shape[0], x.dtype)
            deg = jax.ops.segment_sum(ew, col, num_segments=N)
            dinv = jnp.where(deg > 0, jax.lax.rsqrt(deg), 0.0)
            norm = dinv[row] * dinv[col]
            out = jax.ops.segment_sum(norm[:, None] * xw[row], col, num_segments=N)
            return out + bias
        loops = jnp.arange(N, dtype=edge_index.dtype)
        row = jnp.concatenate([edge_index[0], loops])
        col = jnp.concatenate([edge_index[1], loops])
        h = _layer_norm(x, g0, be0)
        h = _gcn_conv(h, row, col, W0, b0) + h @ lw0.T + lb0
        h = jax.nn.relu(h)
        x_final = h
        h = _layer_norm(h, g1, be1)
        h = _gcn_conv(h, row, col, W1, b1) + h @ lw1.T + lb1
        h = jax.nn.relu(h)
        x_final = x_final + h
        return x_final @ pw.T + pb

    def _L1_gnn_ref(node_feats, edge_attrs, edge_feats, edge_index, W_up0, W_up1, W_mlp1, W_mlp2, W_mlp3, W_mlp4, W_out0, W_out1):
        import jax, jax.numpy as jnp
        import numpy as np
        MUL = 128
        N_NODES = 1250
        N_EDGES = 20000
        R_BASIS = 8
        HIDDEN = 64
        W_NUMEL = 4 * MUL
        SQRT3 = 3.0 ** 0.5
        SILU_2MOM = 1.679177
        AVG_NUM_NEIGHBORS = 10.0

        def _lin_irreps(x0, x1, W0, W1):
            y0 = x0 @ W0 / jnp.sqrt(jnp.float32(W0.shape[0]))
            y1 = jnp.einsum('num,uv->nvm', x1, W1) / jnp.sqrt(jnp.float32(W1.shape[0]))
            return (y0, y1)

        def _forward(node_feats, edge_attrs, edge_feats, edge_index, W_up0, W_up1, W_mlp1, W_mlp2, W_mlp3, W_mlp4, W_out0, W_out1):
            num_nodes = node_feats.shape[0]
            sender, receiver = (edge_index[0], edge_index[1])
            x0 = node_feats[:, :MUL]
            x1 = node_feats[:, MUL:].reshape(num_nodes, MUL, 3)
            x0, x1 = _lin_irreps(x0, x1, W_up0, W_up1)
            h = edge_feats
            for W in (W_mlp1, W_mlp2, W_mlp3):
                h = SILU_2MOM * jax.nn.silu(h @ W / jnp.sqrt(jnp.float32(W.shape[0])))
            tpw = h @ W_mlp4 / jnp.sqrt(jnp.float32(W_mlp4.shape[0]))
            w1, w2, w3, w4 = jnp.split(tpw, 4, axis=-1)
            s0 = x0[sender]
            s1 = x1[sender]
            y0 = edge_attrs[:, 0:1]
            y1 = edge_attrs[:, 1:4]
            p1 = w1 * s0 * y0
            p2 = (w2 * s0)[:, :, None] * y1[:, None, :]
            p3 = w3[:, :, None] * s1 * y0[:, None, :]
            p4 = w4 * jnp.einsum('eum,em->eu', s1, y1) / SQRT3
            m0 = jnp.concatenate([p1, p4], axis=-1)
            m1 = jnp.concatenate([p2, p3], axis=1)
            msg0 = jax.ops.segment_sum(m0, receiver, num_segments=num_nodes)
            msg1 = jax.ops.segment_sum(m1, receiver, num_segments=num_nodes)
            o0, o1 = _lin_irreps(msg0, msg1, W_out0, W_out1)
            out = jnp.concatenate([o0, o1.reshape(num_nodes, 3 * MUL)], axis=-1)
            return out / AVG_NUM_NEIGHBORS
        return _forward(node_feats, edge_attrs, edge_feats, edge_index, W_up0, W_up1, W_mlp1, W_mlp2, W_mlp3, W_mlp4, W_out0, W_out1)
    edge_index = jnp.stack([src, dst])
    h = jnp.maximum(_layernorm(x, axis=-1), 0.0)
    x = x + _L0_gnn_ref(h, edge_index, L0_gnn_W0, L0_gnn_b0, L0_gnn_lw0, L0_gnn_lb0, L0_gnn_g0, L0_gnn_be0, L0_gnn_W1, L0_gnn_b1, L0_gnn_lw1, L0_gnn_lb1, L0_gnn_g1, L0_gnn_be1, L0_gnn_pw, L0_gnn_pb)
    h = jnp.maximum(_layernorm(x, axis=-1), 0.0)
    x = x + _L1_gnn_ref(h, edge_attr_4, edge_attr_8, edge_index, L1_gnn_W_up0, L1_gnn_W_up1, L1_gnn_W_mlp1, L1_gnn_W_mlp2, L1_gnn_W_mlp3, L1_gnn_W_mlp4, L1_gnn_W_out0, L1_gnn_W_out1)
    return x

_drawn_inputs = setup_inputs


def setup_inputs(seed=0):
    import zlib

    import numpy as np

    out = dict(_drawn_inputs(seed))
    spreads = {'L0_gnn_b0': (0.0, 0.1),
     'L0_gnn_lb0': (0.0, 0.1),
     'L0_gnn_g0': (1.0, 0.2),
     'L0_gnn_be0': (0.0, 0.1),
     'L0_gnn_b1': (0.0, 0.1),
     'L0_gnn_lb1': (0.0, 0.1),
     'L0_gnn_g1': (1.0, 0.534),
     'L0_gnn_be1': (0.0, 0.381),
     'L0_gnn_pb': (0.0, 0.1)}
    factors = {}
    for name, (base, spread) in spreads.items():
        noise = np.random.default_rng([zlib.crc32(name.encode()), seed]).standard_normal(out[name].shape)
        drawn = base * np.exp(spread * noise) if base else spread * noise
        out[name] = jnp.asarray(drawn.astype(out[name].dtype))
    for name, factor in factors.items():
        out[name] = (out[name] * factor).astype(out[name].dtype)
    return out
```

```python
from contextlib import ExitStack

import concourse.bass as bass
from concourse import mybir

P = 128
N, D, E = 6250, 512, 100000
NW = (N + P - 1) // P
NPAD = NW * P
TAIL = N - (NW - 1) * P
NT = 784
NG2, NG4 = NT // 2, NT // 4
KC = D // P
HID = 64
RB = 8
EPS = 1e-5
SILU_2MOM = 1.679177
AVG = 10.0

ALU = mybir.AluOpType
ACT = mybir.ActivationFunctionType
F32 = mybir.dt.float32
BF16 = mybir.dt.bfloat16
I32 = mybir.dt.int32
X = mybir.AxisListType.X


def build(nc, a, out):
    with ExitStack() as ctx:
        def sb(name, shape, dt=F32):
            return ctx.enter_context(nc.sbuf_tensor(name, shape, dt))

        def sem(name):
            return ctx.enter_context(nc.semaphore(name))

        def dram(name, shape, dt=F32):
            return nc.dram_tensor(name, shape, dt).ap()

        hid_d = dram("hid_d", (NG2, P, P))
        tab_d = [dram("tab0_d", (NPAD, D)), dram("tab1_d", (NPAD, D))]
        r0_d = dram("r0_d", (NPAD, D))
        x1_d = dram("x1_d", (NPAD, D))
        up_d = dram("up_d", (NPAD, D))
        ext_d = dram("ext_d", (2, NG2))
        rng_d = dram("rng_d", (NW, 4), I32)

        bank = [ctx.enter_context(nc.psum_tensor(f"bank{i}", [P, D], F32)) for i in range(8)]

        src_i = sb("src_i", [P, NT], I32)
        dst_f = sb("dst_f", [P, NT])
        y_t = sb("y_t", [P, NT * 4])
        ident = sb("ident", [P, P])
        iota = sb("iota", [P, P])
        iota_w = sb("iota_w", [P, P])
        zeros = sb("zeros", [P, D], BF16)
        eps = sb("eps", [P, 1])
        rdeg = sb("rdeg", [P, NW])
        dinv = sb("dinv", [P, NW])
        rng = sb("rng", [1, 4 * NW], I32)
        dense_w = sb("dense_w", [P, 5, KC, D])
        W = {k: dense_w[:, i, :, :] for i, k in enumerate(("W0", "lw0", "W1", "lw1", "pw"))}
        wup = sb("wup", [P, 2, P])
        w1 = sb("w1", [2 * RB, P])
        w2 = sb("w2", [P, P])
        w3 = sb("w3", [P, P])
        w4 = sb("w4", [P, D])
        wo = sb("wo", [P, 4, P])
        bia = {k: sb("v_" + k, [P, D]) for k in ("b0", "lb0", "g0", "be0", "b1", "lb1", "g1", "be1", "pb")}

        dst_i = sb("dst_i", [P, NT], I32)
        hi_i = sb("hi_i", [P, NT], I32)
        lo_i = sb("lo_i", [P, NT], I32)
        hi_f = sb("hi_f", [P, NT])
        lo_f = sb("lo_f", [P, NT])
        ohl = sb("ohl", [P, 2, 8, P], BF16)
        ohh = sb("ohh", [P, 2, 8, NW], BF16)
        dst_g = sb("dst_g", [NG2 // 4, 4 * 256], I32)
        ext = sb("ext", [NG2 // 4, 2, 4])
        extb = sb("extb", [NW, 2, NG2])
        ext4 = sb("ext4", [NW, 2, NG4])
        asc = sb("asc", [NW, NG2])
        asc_i = sb("asc_i", [NW, NG2], I32)
        rtmp = sb("rtmp", [NW, NG2])
        rtmp2 = sb("rtmp2", [NW, NG2])
        wlo = sb("wlo", [NW, 1])
        wlo_i = sb("wlo_i", [NW, 1], I32)
        rcol = sb("rcol", [NW, 8])
        rcol_i = sb("rcol_i", [NW, 4], I32)
        iota_i = sb("iota_i", [P, P], I32)
        pid_i = sb("pid_i", [P, 1], I32)
        pid = sb("pid", [P, 1])
        ef = sb("ef", [2 * RB, 2, D])
        hA = sb("hA", [P, 2, D])
        hB = sb("hB", [P, 2, D])
        hC = sb("hC", [P, 2, D])

        xin = sb("xin", [P, 2, D])
        hrel = sb("hrel", [P, 2, D])
        tn = sb("tn", [P, 2, D])
        tout = sb("tout", [P, 2, D])
        st = sb("st", [P, 2, 6])
        mv = sb("mv", [P, 2, 8])

        ring = sb("ring", [P, 4, D])
        oh = sb("oh", [P, 4, P])
        idx = sb("idx", [P, 4], I32)
        tw = sb("tw", [P, D])
        tw2 = sb("tw2", [P, D])
        hw = sb("hw", [P, D])
        agg = sb("agg", [P, D])
        AT = sb("AT", [P, 8, P])
        yb = sb("yb", [P, D])
        r = sb("r", [P, D])
        r0w = sb("r0w", [P, D])
        xs = sb("xs", [P, D])
        xT = sb("xT", [P, KC, P])
        xw = sb("xw", [P, D])
        x1 = sb("x1", [P, D])
        hT = sb("hT", [P, KC, P])
        uo = sb("uo", [P, D])

        msg = dense_w[:, 0:2, :, :].rearrange("p a c n -> p (a c n)")
        hid = sb("hid", [P, P])
        yg = sb("yg", [P, 8])
        w13 = sb("w13", [P, 2, 256])
        t2 = sb("t2", [P, 2, P])
        q0 = sb("q0", [P, 2, P])
        q1 = sb("q1", [P, 2, P])
        q2 = sb("q2", [P, 2, P])
        mA, mB, mT = agg, hw, AT

        def s(name):
            return sem(name)

        s_edge, s_small, s_big = s("edges_in"), s("small_weights_in"), s("big_weights_in")
        s_gext, s_extst, s_extld, s_rst, s_rld = (s("ext_ready"), s("ext_stored"), s("ext_loaded"),
                                                  s("ranges_stored"), s("ranges_loaded"))
        s_cst, s_wz, s_wsc, s_rcol = s("constants_ready"), s("weights_zeroed"), s("weights_scaled"), s("ranges_ready")
        ef_in = [s(f"ef_in{i}") for i in range(2)]
        hid_out = [s(f"hid_out{i}") for i in range(2)]
        m1, m2, m3 = s("radial1_sum"), s("radial2_sum"), s("radial3_sum")
        a1, a2, a3 = s("radial1_act"), s("radial2_act"), s("radial3_act")
        oh_rdy, oh_used = s("degree_onehot_ready"), s("degree_onehot_used")
        deg_sum, deg_ready, deg_sq = s("degree_summed"), s("dinv_ready"), s("degree_root")
        x_in = [s(f"x_in{i}") for i in range(2)]
        t_st = [s(f"table0_stored{i}") for i in range(2)]
        n_st1, n_sd1, n_rs1, n_h, n_st2, n_sd2, n_rs2, n_t, n_out = (
            s("norm_stats1"), s("norm_std1"), s("norm_scale1"), s("norm_relu"), s("norm_stats2"),
            s("norm_std2"), s("norm_scale2"), s("norm_table_scaled"), s("norm_table_ready"))

        def peeled(eng, stages):
            depth = max(d for d, _ in stages)
            for w in range(depth + 1):
                for d, f in stages:
                    if w - d >= 0:
                        f(w - d)
            with eng.Fori(depth + 1, NW) as w:
                for d, f in stages:
                    f(w - d)
            for w in range(NW, NW + depth):
                for d, f in stages:
                    if w - d < NW:
                        f(w - d)

        def after(eng, sm, w, per=1):
            if isinstance(w, int):
                if w > 0:
                    eng.wait_ge(sm, w * per)
            else:
                eng.wait_ge(sm, w * per)

        def looped(eng, body, n):
            body(0)
            with eng.Fori(1, n) as i:
                body(i)

        def rows(t, w):
            return t[w * P:(w + 1) * P, :] if isinstance(w, int) else t[bass.ds(w * P, P), :]

        def col(t, w):
            return t[:, w:w + 1] if isinstance(w, int) else t[:, bass.ds(w, 1)]

        def window_range(eng, w, kind):
            top = NG4 if kind == 0 else NG2
            at = w * 4 + 2 * kind
            if isinstance(w, int):
                la, ha = rng[0:1, at:at + 1], rng[0:1, at + 1:at + 2]
            else:
                la, ha = rng[0:1, bass.ds(at, 1)], rng[0:1, bass.ds(w * 4 + (2 * kind + 1), 1)]
            return (eng.value_load(la, min_val=0, max_val=top - 1 - kind),
                    eng.value_load(ha, min_val=1, max_val=top))

        block = ctx.enter_context(nc.Block())

        def gcn_sems(L):
            names = ("idx_ready", "onehot_a", "onehot_b", "sum_done", "agg_ready", "self_in", "self_scaled",
                     "turned", "at_a", "at_b", "dense_done", "y_read", "relu_done", "r_stored", "tab_stored",
                     "stats", "std", "scale", "tn", "tout", "r0_in", "xs_ready", "xs_turned", "xT_ready",
                     "proj_done", "x_in", "x1_ready", "x1_stored", "h_ready", "h_turned", "hT_ready", "up_done",
                     "up_ready", "up_stored")
            S = {k: s(f"gcn{L}_{k}") for k in names}
            S["got"] = [s(f"gcn{L}_gathered{k}") for k in range(4)]
            S["used"] = [s(f"gcn{L}_slot_used{k}") for k in range(4)]
            return S

        G = [gcn_sems(0), gcn_sems(1)]
        w_bank = [[bank[2], bank[3]], [bank[7], bank[5]]]
        m_bank = [bank[4], bank[6]]
        M = {k: s("tp_" + k) for k in (
            "idx_ready", "hid_in", "w_done", "y_ready", "w13", "t2", "q0", "p2", "u_used",
            "psum_read_act", "msg_ready", "onehot", "seg_done", "sum_done", "mA", "mB", "turned", "mT_a", "mT_b",
            "o_done", "x1_in", "out_ready", "stored", "msgs_used")}
        M["got"] = [s(f"tp_gathered{k}") for k in range(2)]

        @block.sync
        def _(sp):
            for t, k in ((src_i, "src_t"), (dst_i, "dst_t"), (dst_g, "dst_g"), (y_t, "ea_t")):
                sp.dma_start(t[:, :], a[k]).then_inc(s_edge, 16)
            for k in bia:
                sp.dma_start(bia[k][:, :], a[k].rearrange("(a d) -> a d", a=1).broadcast_to([P, D])).then_inc(s_small, 16)
            sp.dma_start(wup[:, 0, :], a["W_up0"]).then_inc(s_small, 16)
            sp.dma_start(wup[:, 1, :], a["W_up1"]).then_inc(s_small, 16)
            sp.dma_start(wo[:, 0:2, :], a["W_out0"].rearrange("(c p) n -> p c n", p=P)).then_inc(s_small, 16)
            sp.dma_start(wo[:, 2:4, :], a["W_out1"].rearrange("(c p) n -> p c n", p=P)).then_inc(s_small, 16)
            sp.wait_ge(s_wz, 3)
            for t, k, n in ((w1, "W_mlp1", RB), (w2, "W_mlp2", HID), (w3, "W_mlp3", HID)):
                for h in range(2):
                    sp.dma_start(t[h * n:(h + 1) * n, h * HID:(h + 1) * HID], a[k]).then_inc(s_small, 16)
            for h in range(2):
                for c, f in enumerate((0, 2, 1, 3)):
                    sp.dma_start(w4[h * HID:(h + 1) * HID, c * P:(c + 1) * P],
                                 a["W_mlp4"][:, f * P:(f + 1) * P]).then_inc(s_small, 16)
            sp.wait_ge(s_gext, 1)
            sp.dma_start(ext_d.rearrange("a (p q) -> p a q", q=4), ext[:, :, :]).then_inc(s_extst, 16)
            for k in W:
                sp.dma_start(W[k][:, :, :], a[k].rearrange("(c p) n -> p c n", p=P)).then_inc(s_big, 16)
            sp.wait_ge(s_extst, 16)
            sp.dma_start(extb[:, :, :], ext_d.rearrange("(o a) g -> o a g", o=1).broadcast_to([NW, 2, NG2])).then_inc(s_extld, 16)
            sp.wait_ge(s_rcol, 1)
            sp.dma_start(rng_d, rcol_i[:, :]).then_inc(s_rst, 16)
            sp.wait_ge(s_rst, 16)
            sp.dma_start(rng[:, :], rng_d.rearrange("(o w) k -> o (w k)", o=1)).then_inc(s_rld, 16)

            sp.wait_ge(s_wsc, 1)
            def radial(j):
                for b in range(2):
                    if not isinstance(j, int):
                        sp.wait_ge(m1, j * 2 - 1 + b)
                    sp.dma_start(ef[:, b, :], a["ef_t"][:, bass.ds((j * 2 + b) * D, D)]).then_inc(ef_in[b], 16)
                for b in range(2):
                    sp.wait_ge(a3, j * 2 + 1 + b)
                    sp.dma_start(hid_d[bass.ds((j * 2 + b) * 4, 4), :, :].rearrange("g p e -> p g e"),
                                 hC[:, b, :].rearrange("p (g e) -> p g e", g=4)).then_inc(hid_out[b], 16)

            looped(sp, radial, NG2 // 8)

            def norm(j):
                for b in range(2):
                    if not isinstance(j, int):
                        sp.wait_ge(n_h, j * 2 - 1 + b)
                    sp.dma_start(xin[:, b, :], a["x"][bass.ds((j * 2 + b) * P, P), :]).then_inc(x_in[b], 16)
                for b in range(2):
                    sp.wait_ge(n_out, j * 2 + 1 + b)
                    sp.dma_start(tab_d[0][bass.ds((j * 2 + b) * P, P), :], tout[:, b, :]).then_inc(t_st[b], 16)

            looped(sp, norm, NW // 2)
            sp.wait_ge(n_h, NW - 2)
            sp.dma_start(xin[0:TAIL, 0, :], a["x"][N - TAIL:N, :]).then_inc(x_in[0], 16)
            sp.wait_ge(n_out, NW)
            sp.dma_start(tab_d[0][(NW - 1) * P:, :], tout[:, 0, :]).then_inc(t_st[0], 16)
            sp.wait_ge(t_st[0], 16 * (NW // 2 + 1))
            sp.wait_ge(t_st[1], 16 * (NW // 2))

            for L in range(2):
                S = G[L]

                def self_rows(w, S=S, L=L):
                    after(sp, S["self_scaled"], w)
                    sp.dma_start(tw[:, :], rows(tab_d[L], w)).then_inc(S["self_in"], 16)

                def store_r(w, S=S):
                    sp.wait_ge(S["relu_done"], w + 1)
                    sp.dma_start(rows(r0_d, w), r[:, :]).then_inc(S["r_stored"], 16)

                def store_tab(w, S=S):
                    sp.wait_ge(S["tout"], w + 1)
                    sp.dma_start(rows(tab_d[1], w), tout[:, 0, :]).then_inc(S["tab_stored"], 16)

                def load_r0(w, S=S):
                    after(sp, S["xs_ready"], w)
                    sp.dma_start(r0w[:, :], rows(r0_d, w)).then_inc(S["r0_in"], 16)

                def load_x(w, S=S):
                    after(sp, S["x1_ready"], w)
                    if isinstance(w, int) and w == NW - 1:
                        sp.dma_start(xw[0:TAIL, :], a["x"][N - TAIL:N, :]).then_inc(S["x_in"], 16)
                    else:
                        sp.dma_start(xw[:, :], rows(a["x"], w)).then_inc(S["x_in"], 16)

                def store_x1(w, S=S):
                    sp.wait_ge(S["x1_ready"], w + 1)
                    sp.dma_start(rows(x1_d, w), x1[:, :]).then_inc(S["x1_stored"], 16)

                def store_up(w, S=S):
                    sp.wait_ge(S["up_ready"], w + 1)
                    sp.dma_start(rows(up_d, w), uo[:, :]).then_inc(S["up_stored"], 16)

                if L == 0:
                    peeled(sp, [(0, self_rows), (2, store_r), (2, store_tab)])
                    sp.wait_ge(S["r_stored"], 16 * NW)
                    sp.wait_ge(S["tab_stored"], 16 * NW)
                else:
                    peeled(sp, [(0, self_rows), (2, load_r0), (2, load_x), (3, store_up), (2, store_x1)])
                    sp.wait_ge(S["x1_stored"], 16 * NW)
                    sp.wait_ge(S["up_stored"], 16 * NW)

            sp.wait_ge(hid_out[0], 16 * (NG2 // 8))
            sp.wait_ge(hid_out[1], 16 * (NG2 // 8))
            c = sp.alloc_register("sp_tp_count")
            sp.reg_mov(c, 1)

            def hidden(w):
                lo, hi = window_range(sp, w, 1)
                with sp.Fori(lo, hi) as g:
                    sp.wait_ge(M["w_done"], c)
                    sp.dma_start(hid[:, :], hid_d[bass.ds(g, 1), :, :].rearrange("g p e -> p (g e)")).then_inc(M["hid_in"], 16)
                    sp.reg_add(c, c, 1)

            def load_x1(w):
                after(sp, M["out_ready"], w)
                sp.dma_start(xw[:, :], rows(x1_d, w)).then_inc(M["x1_in"], 16)

            def store_out(w):
                sp.wait_ge(M["out_ready"], w + 1)
                if isinstance(w, int) and w == NW - 1:
                    sp.dma_start(out[N - TAIL:N, :], x1[0:TAIL, :]).then_inc(M["stored"], 16)
                else:
                    sp.dma_start(rows(out, w), x1[:, :]).then_inc(M["stored"], 16)

            peeled(sp, [(0, hidden), (2, store_out), (1, load_x1)])
            sp.wait_ge(M["stored"], 16 * NW)

        @block.gpsimd
        def _(g_):
            g_.iota(iota_i[:, :], [[1, P]], base=0, channel_multiplier=0).then_inc(s_cst, 1)
            g_.iota(pid_i[:, :], [[1, 1]], base=0, channel_multiplier=1).then_inc(s_cst, 1)
            g_.iota(asc_i[:, :], [[1, NG2]], base=1, channel_multiplier=0).then_inc(s_cst, 1)
            g_.iota(wlo_i[:, :], [[1, 1]], base=0, channel_multiplier=P).then_inc(s_cst, 1)
            g_.memset(eps[:, :], EPS).then_inc(s_cst, 1)
            g_.memset(zeros[:, :], 0.0).then_inc(s_cst, 1)
            g_.memset(w1[:, :], 0.0).then_inc(s_wz, 1)
            g_.memset(w2[:, :], 0.0).then_inc(s_wz, 1)
            g_.memset(w3[:, :], 0.0).then_inc(s_wz, 1)

            def gathers(S, table, name, kind, free):
                pairs = len(free)
                c = g_.alloc_register(f"pool_{name}_index")
                cf = [g_.alloc_register(f"pool_{name}_pair{h}") for h in range(pairs)]
                g_.reg_mov(c, 1)
                for h in range(pairs):
                    g_.reg_mov(cf[h], 1)

                def body(w):
                    lo, hi = window_range(g_, w, kind)
                    with g_.Fori(lo, hi) as g:
                        for h in range(pairs):
                            g_.wait_ge(free[h], cf[h])
                            g_.reg_add(cf[h], cf[h], 1)
                            g_.tensor_copy(idx[:, 2 * h:2 * h + 2],
                                           src_i[:, bass.ds(g * (2 * pairs) + 2 * h, 2)]).then_inc(S["idx_ready"], 1)
                            g_.wait_ge(S["idx_ready"], c)
                            g_.reg_add(c, c, 1)
                            for k in (2 * h, 2 * h + 1):
                                g_.indirect_dma_start(ring[:, k, :], None, table,
                                                      bass.IndirectOffsetOnAxis(idx[:, k:k + 1], 0)).then_inc(S["got"][k], 16)
                peeled(g_, [(0, body)])

            g_.wait_ge(s_edge, 64)
            g_.wait_ge(s_rld, 16)
            g_.wait_ge(t_st[0], 16 * (NW // 2 + 1))
            g_.wait_ge(t_st[1], 16 * (NW // 2))
            gathers(G[0], tab_d[0], "gcn0", 0, [G[0]["used"][1], G[0]["used"][3]])
            g_.wait_ge(G[0]["tab_stored"], 16 * NW)
            gathers(G[1], tab_d[1], "gcn1", 0, [G[1]["used"][1], G[1]["used"][3]])
            g_.wait_ge(G[1]["up_stored"], 16 * NW)
            gathers(M, up_d, "tp", 1, [M["u_used"]])

        @block.scalar
        def _(ac):
            ac.wait_ge(s_small, 16 * (len(bia) + 4 + 6 + 8))
            ac.mul(w1[:, :], w1[:, :], RB ** -0.5)
            for t in (w2, w3):
                ac.mul(t[:, :], t[:, :], SILU_2MOM * HID ** -0.5)
            ac.mul(w4[:, 0:3 * P], w4[:, 0:3 * P], SILU_2MOM * HID ** -0.5)
            ac.mul(w4[:, 3 * P:], w4[:, 3 * P:], SILU_2MOM * HID ** -0.5 * 3 ** -0.5)
            ac.mul(wup[:, :, :], wup[:, :, :], P ** -0.5)
            ac.mul(wo[:, :, :], wo[:, :, :], (2 * P) ** -0.5 / AVG)
            ac.drain()
            ac.nop().then_inc(s_wsc, 1)
            def radial(j):
                for b in range(2):
                    ac.wait_ge(m1, j * 2 + 1 + b)
                    ac.activation(hA[:, b, :], bank[0 + b][:, :], ACT.Silu).then_inc(a1, 1)
                for b in range(2):
                    ac.wait_ge(m2, j * 2 + 1 + b)
                    ac.activation(hB[:, b, :], bank[2 + b][:, :], ACT.Silu).then_inc(a2, 1)
                for b in range(2):
                    after(ac, hid_out[b], j, 16)
                    ac.wait_ge(m3, j * 2 + 1 + b)
                    ac.activation(hC[:, b, :], bank[4 + b][:, :], ACT.Silu).then_inc(a3, 1)

            looped(ac, radial, NG2 // 8)
            ac.wait_ge(deg_ready, 1)
            ac.activation(rdeg[:, :], rdeg[:, :], ACT.Sqrt).then_inc(deg_sq, 1)

            def norm_tiles(base, bs):
                for b in bs:
                    ac.wait_ge(n_st1, base + 1 + b)
                    ac.activation(mv[:, b, 2:3], mv[:, b, 1:2], ACT.Sqrt, bias=eps[:, 0:1]).then_inc(n_sd1, 1)
                for b in bs:
                    ac.wait_ge(n_rs1, base + 1 + b)
                    ac.activation(hrel[:, b, :], xin[:, b, :], ACT.Relu, bias=mv[:, b, 4:5],
                                  scale=mv[:, b, 3:4]).then_inc(n_h, 1)
                for b in bs:
                    ac.wait_ge(n_st2, base + 1 + b)
                    ac.activation(mv[:, b, 2:3], mv[:, b, 1:2], ACT.Sqrt, bias=eps[:, 0:1]).then_inc(n_sd2, 1)
                for b in bs:
                    ac.wait_ge(n_rs2, base + 1 + b)
                    ac.activation(tn[:, b, :], hrel[:, b, :], ACT.Identity, bias=mv[:, b, 4:5],
                                  scale=mv[:, b, 3:4]).then_inc(n_t, 1)

            with ac.Fori(0, NW // 2) as j:
                norm_tiles(j * 2, (0, 1))
            norm_tiles(NW - 1, (0,))
            ac.wait_ge(s_rld, 16)

            for L in range(2):
                S = G[L]

                def self_terms(w, S=S):
                    sp_in = S["self_in"]
                    ac.wait_ge(sp_in, (w + 1) * 16)
                    after(ac, S["agg_ready"], w)
                    ac.mul(tw2[:, :], tw[:, :], col(dinv, w))
                    after(ac, S["turned"], w)
                    ac.mul(hw[:, :], tw[:, :], col(rdeg, w)).then_inc(S["self_scaled"], 1)

                def copy_at(w, S=S):
                    ac.wait_ge(S["turned"], w + 1)
                    after(ac, S["dense_done"], w)
                    ac.copy(AT[:, 0:4, :], bank[1][:, :].rearrange("p (c n) -> p c n", c=4)).then_inc(S["at_a"], 1)

                def relu_r(w, S=S, L=L):
                    ac.wait_ge(S["y_read"], w + 1)
                    if L == 0:
                        after(ac, S["r_stored"], w, 16)
                    else:
                        after(ac, S["xs_ready"], w)
                    ac.activation(r[:, :], yb[:, :], ACT.Relu).then_inc(S["relu_done"], 1)

                def std(w, S=S):
                    ac.wait_ge(S["stats"], w + 1)
                    ac.activation(mv[:, 0, 2:3], mv[:, 0, 1:2], ACT.Sqrt, bias=eps[:, 0:1]).then_inc(S["std"], 1)

                def scaled(w, S=S):
                    ac.wait_ge(S["scale"], w + 1)
                    ac.activation(tn[:, 0, :], r[:, :], ACT.Identity, bias=mv[:, 0, 4:5],
                                  scale=mv[:, 0, 3:4]).then_inc(S["tn"], 1)

                def copy_xT(w, S=S):
                    ac.wait_ge(S["xs_turned"], w + 1)
                    after(ac, S["proj_done"], w)
                    ac.copy(xT[:, :, :], bank[4][:, :].rearrange("p (c n) -> p c n", c=4)).then_inc(S["xT_ready"], 1)

                def relu_h(w, S=S):
                    ac.wait_ge(S["scale"], w + 1)
                    after(ac, S["h_turned"], w)
                    ac.activation(hrel[:, 0, :], x1[:, :], ACT.Relu, bias=mv[:, 0, 4:5],
                                  scale=mv[:, 0, 3:4]).then_inc(S["h_ready"], 1)

                def copy_hT(w, S=S):
                    ac.wait_ge(S["h_turned"], w + 1)
                    after(ac, S["up_done"], w)
                    ac.copy(hT[:, :, :], bank[6][:, :].rearrange("p (c n) -> p c n", c=4)).then_inc(S["hT_ready"], 1)

                def up_out(w, S=S):
                    ac.wait_ge(S["up_done"], w + 1)
                    after(ac, S["up_stored"], w, 16)
                    ac.copy(uo[:, :], bank[7][:, :]).then_inc(S["up_ready"], 1)

                if L == 0:
                    peeled(ac, [(1, copy_at), (0, self_terms), (2, relu_r), (2, std), (2, scaled)])
                else:
                    peeled(ac, [(3, copy_hT), (1, copy_at), (0, self_terms), (3, up_out), (2, relu_r),
                                (2, copy_xT), (2, std), (2, relu_h)])

            c = ac.alloc_register("act_tp_count")
            cg = [ac.alloc_register(f"act_tp_got{k}") for k in range(2)]
            ac.reg_mov(c, 1)
            ac.reg_mov(cg[0], 16)
            ac.reg_mov(cg[1], 16)

            def weigh(w):
                lo, hi = window_range(ac, w, 1)
                with ac.Fori(lo, hi) as g:
                    n = ac.snap(c)
                    ac.wait_ge(M["msg_ready"], n)
                    ac.copy(yg[:, :], y_t[:, bass.ds(g * 8, 8)]).then_inc(M["y_ready"], 1)
                    ac.drain()
                    for k in range(2):
                        ac.wait_ge(M["got"][k], cg[k])
                        ac.reg_add(cg[k], cg[k], 16)
                        ac.mul(q0[:, k, :], ring[:, k, P:2 * P], yg[:, 4 * k + 1:4 * k + 2]).then_inc(M["q0"], 1)
                    ac.wait_ge(M["w_done"], n + 1)
                    for k in range(2):
                        ac.mul(w13[:, k, :], w_bank[k][0][:, 0:2 * P], yg[:, 4 * k:4 * k + 1]).then_inc(M["w13"], 1)
                    ac.wait_ge(M["t2"], n)
                    ac.wait_ge(M["seg_done"], n)
                    for k in range(2):
                        for m in range(3):
                            ins = ac.mul(msg[:, bass.ds((n % 2) * (4 * D) + (k * 2 * D + D + P + m * P), P)], t2[:, k, :],
                                         yg[:, 4 * k + 1 + m:4 * k + 2 + m])
                    ins.then_inc(M["p2"], 1)
                    ac.reg_add(c, c, 1)

            def keep_a(w):
                ac.wait_ge(M["sum_done"], w + 1)
                after(ac, M["turned"], w)
                ac.copy(mA[:, :], bank[0][:, :]).then_inc(M["mA"], 1)

            def copy_mT(w):
                ac.wait_ge(M["turned"], w + 1)
                after(ac, M["o_done"], w)
                ac.copy(mT[:, 0:4, :], bank[4][:, :].rearrange("p (c n) -> p c n", c=4)).then_inc(M["mT_a"], 1)

            peeled(ac, [(0, weigh), (1, copy_mT), (0, keep_a)])

        @block.vector
        def _(ve):
            ve.wait_ge(s_edge, 64)
            ve.tensor_scalar(hi_i[:, :], dst_i[:, :], 7, None, ALU.arith_shift_right)
            ve.tensor_scalar(lo_i[:, :], dst_i[:, :], 127, None, ALU.bitwise_and)
            ve.tensor_copy(dst_f[:, :], dst_i[:, :])
            for h in range(2):
                dg = dst_g[:, :].rearrange("p (q e) -> p q e", q=4)
                ve.tensor_reduce(ext[:, h, :], dg, X, ALU.min if h == 0 else ALU.max)
            ve.drain()
            ve.nop().then_inc(s_gext, 1)
            ve.tensor_copy(hi_f[:, :], hi_i[:, :])
            ve.tensor_copy(lo_f[:, :], lo_i[:, :])
            ve.wait_ge(s_cst, 6)
            ve.tensor_copy(iota[:, :], iota_i[:, :])
            ve.tensor_copy(pid[:, :], pid_i[:, :])
            ve.tensor_copy(asc[:, :], asc_i[:, :])
            ve.tensor_copy(wlo[:, :], wlo_i[:, :])
            ve.drain()
            ve.tensor_scalar(ident[:, :], iota[:, :], pid[:, 0:1], None, ALU.is_equal)
            ve.wait_ge(s_small, 16 * (len(bia) + 4 + 6 + 8))
            ve.tensor_tensor(bia["b0"][:, :], bia["b0"][:, :], bia["lb0"][:, :], ALU.add)
            ve.tensor_tensor(bia["b1"][:, :], bia["b1"][:, :], bia["lb1"][:, :], ALU.add)

            ve.wait_ge(s_extld, 16)
            for h, op in ((0, ALU.min), (1, ALU.max)):
                ve.tensor_reduce(ext4[:, h, :], extb[:, h, :].rearrange("p (g q) -> p g q", q=2), X, op)
            ve.tensor_scalar(rcol[:, 4:5], wlo[:, :], float(P), None, ALU.add)
            ve.drain()
            for kind, (ex, ng) in enumerate(((ext4, NG4), (extb, NG2))):
                ve.tensor_scalar(rtmp[:, 0:ng], asc[:, 0:ng], -1.0, float(ng + 1), ALU.mult, ALU.add)
                ve.drain()
                ve.scalar_tensor_tensor(out=rtmp2[:, 0:ng], in0=ex[:, 1, :], scalar=wlo[:, 0:1], in1=rtmp[:, 0:ng],
                                        op0=ALU.is_ge, op1=ALU.mult)
                ve.drain()
                ve.tensor_reduce(rcol[:, 5:6], rtmp2[:, 0:ng], X, ALU.max)
                ve.drain()
                ve.tensor_scalar(rcol[:, 6:7], rcol[:, 5:6], -1.0, float(ng), ALU.mult, ALU.add)
                ve.scalar_tensor_tensor(out=rtmp2[:, 0:ng], in0=ex[:, 0, :], scalar=rcol[:, 4:5], in1=asc[:, 0:ng],
                                        op0=ALU.is_lt, op1=ALU.mult)
                ve.drain()
                ve.tensor_scalar(rcol[:, 2 * kind:2 * kind + 1], rcol[:, 6:7], float(ng - 1 - kind), None, ALU.min)
                ve.tensor_reduce(rcol[:, 5:6], rtmp2[:, 0:ng], X, ALU.max)
                ve.drain()
                ve.scalar_tensor_tensor(out=rcol[:, 2 * kind + 1:2 * kind + 2], in0=rcol[:, 2 * kind:2 * kind + 1],
                                        scalar=float(1 + kind), in1=rcol[:, 5:6], op0=ALU.add, op1=ALU.max)
                ve.drain()
            ve.tensor_copy(rcol_i[:, :], rcol[:, 0:4]).then_inc(s_rcol, 1)

            def degree_onehots(j):
                for b in range(2):
                    if not isinstance(j, int):
                        ve.wait_ge(oh_used, j * 2 - 1 + b)
                    at = bass.ds((j * 2 + b) * 8, 8)
                    ve.tensor_tensor(ohl[:, b, :, :], iota[:, :].unsqueeze(1).broadcast_to([P, 8, P]),
                                     lo_f[:, at].unsqueeze(2).broadcast_to([P, 8, P]), ALU.is_equal)
                    ve.tensor_tensor(ohh[:, b, :, :], iota[:, 0:NW].unsqueeze(1).broadcast_to([P, 8, NW]),
                                     hi_f[:, at].unsqueeze(2).broadcast_to([P, 8, NW]), ALU.is_equal).then_inc(oh_rdy, 1)

            looped(ve, degree_onehots, NT // 16)
            ve.wait_ge(deg_sum, 1)
            ve.tensor_scalar(rdeg[:, :], bank[6][:, 0:NW], 1.0, None, ALU.add).then_inc(deg_ready, 1)
            ve.wait_ge(deg_sq, 1)
            ve.reciprocal(dinv[:, :], rdeg[:, :])
            ve.drain()

            def stats(src, b):
                ve.bn_stats(st[:, b, :], src)
                ve.drain()
                return ve.bn_aggr(mv[:, b, 0:2], st[:, b, :])

            def scale(b, dcol=None):
                ve.reciprocal(mv[:, b, 3:4], mv[:, b, 2:3])
                ve.drain()
                if dcol is not None:
                    ve.tensor_tensor(mv[:, b, 3:4], mv[:, b, 3:4], dcol, ALU.mult)
                    ve.drain()
                return ve.scalar_tensor_tensor(out=mv[:, b, 4:5], in0=mv[:, b, 0:1], scalar=-1.0, in1=mv[:, b, 3:4],
                                               op0=ALU.mult, op1=ALU.mult)

            def affine(b, dst, g, be, dcol):
                ve.tensor_tensor(tn[:, b, :], tn[:, b, :], g[:, :], ALU.mult)
                ve.drain()
                return ve.scalar_tensor_tensor(out=dst, in0=be[:, :], scalar=dcol, in1=tn[:, b, :],
                                               op0=ALU.mult, op1=ALU.add)

            def norm_tiles(base, j, bs):
                for b in bs:
                    ve.wait_ge(x_in[b], (j + 1) * 16)
                    stats(xin[:, b, :], b).then_inc(n_st1, 1)
                for b in bs:
                    ve.wait_ge(n_sd1, base + 1 + b)
                    scale(b).then_inc(n_rs1, 1)
                for b in bs:
                    ve.wait_ge(n_h, base + 1 + b)
                    stats(hrel[:, b, :], b).then_inc(n_st2, 1)
                for b in bs:
                    ve.wait_ge(n_sd2, base + 1 + b)
                    scale(b, col(dinv, base + b)).then_inc(n_rs2, 1)
                for b in bs:
                    ve.wait_ge(n_t, base + 1 + b)
                    after(ve, t_st[b], j, 16)
                    affine(b, tout[:, b, :], bia["g0"], bia["be0"], col(dinv, base + b)).then_inc(n_out, 1)

            looped(ve, lambda j: norm_tiles(j * 2, j, (0, 1)), NW // 2)
            norm_tiles(NW - 1, NW // 2, (0,))
            ve.wait_ge(s_rld, 16)

            for L in range(2):
                S = G[L]
                c = ve.alloc_register(f"dve_gcn{L}_count")
                ve.reg_mov(c, 1)
                ve.tensor_copy(iota_w[:, :], iota[:, :])

                def onehots(w, S=S, c=c):
                    lo, hi = window_range(ve, w, 0)
                    ve.drain()
                    with ve.Fori(lo, hi) as g:
                        for h in range(2):
                            ve.wait_ge(S["used"][2 * h + 1], c)
                            ve.tensor_tensor(oh[:, 2 * h:2 * h + 2, :], iota_w[:, :].unsqueeze(1).broadcast_to([P, 2, P]),
                                             dst_f[:, bass.ds(g * 4 + 2 * h, 2)].unsqueeze(2).broadcast_to([P, 2, P]),
                                             ALU.is_equal).then_inc(S["onehot_b" if h else "onehot_a"], 1)
                        ve.reg_add(c, c, 1)
                    ve.drain()
                    ve.tensor_scalar(iota_w[:, :], iota_w[:, :], float(P), None, ALU.add)

                def aggregate(w, S=S):
                    ve.wait_ge(S["self_scaled"], w + 1)
                    ve.wait_ge(S["sum_done"], w + 1)
                    after(ve, S["turned"], w)
                    ve.scalar_tensor_tensor(out=agg[:, :], in0=bank[0][:, :], scalar=col(dinv, w), in1=tw2[:, :],
                                            op0=ALU.mult, op1=ALU.add).then_inc(S["agg_ready"], 1)

                def copy_at(w, S=S):
                    ve.wait_ge(S["turned"], w + 1)
                    after(ve, S["dense_done"], w)
                    ve.tensor_copy(AT[:, 4:8, :], bank[2][:, :].rearrange("p (c n) -> p c n", c=4)).then_inc(S["at_b"], 1)

                def add_bias(w, S=S, L=L):
                    ve.wait_ge(S["dense_done"], w + 1)
                    after(ve, S["relu_done"], w)
                    ve.tensor_tensor(yb[:, :], bank[3][:, :], bia["b0" if L == 0 else "b1"][:, :],
                                     ALU.add).then_inc(S["y_read"], 1)

                def second_norm(w, S=S):
                    ve.wait_ge(S["relu_done"], w + 1)
                    stats(r[:, :], 0).then_inc(S["stats"], 1)
                    ve.wait_ge(S["std"], w + 1)
                    scale(0, col(dinv, w)).then_inc(S["scale"], 1)
                    ve.wait_ge(S["tn"], w + 1)
                    after(ve, S["tab_stored"], w, 16)
                    affine(0, tout[:, 0, :], bia["g1"], bia["be1"], col(dinv, w)).then_inc(S["tout"], 1)

                def project_in(w, S=S):
                    ve.wait_ge(S["relu_done"], w + 1)
                    ve.wait_ge(S["r0_in"], (w + 1) * 16)
                    after(ve, S["xs_turned"], w)
                    ve.tensor_tensor(xs[:, :], r[:, :], r0w[:, :], ALU.add).then_inc(S["xs_ready"], 1)

                def residual(w, S=S):
                    ve.wait_ge(S["x_in"], (w + 1) * 16)
                    ve.wait_ge(S["proj_done"], w + 1)
                    after(ve, S["x1_stored"], w, 16)
                    after(ve, S["h_ready"], w)
                    ve.tensor_tensor(x1[:, :], bank[5][:, :], bia["pb"][:, :], ALU.add)
                    ve.drain()
                    ve.tensor_tensor(x1[:, :], x1[:, :], xw[:, :], ALU.add).then_inc(S["x1_ready"], 1)
                    ve.drain()
                    stats(x1[:, :], 0).then_inc(S["stats"], 1)
                    ve.wait_ge(S["std"], w + 1)
                    scale(0).then_inc(S["scale"], 1)

                if L == 0:
                    peeled(ve, [(0, onehots), (2, add_bias), (1, copy_at), (0, aggregate), (2, second_norm)])
                else:
                    peeled(ve, [(0, onehots), (2, add_bias), (1, copy_at), (0, aggregate), (2, project_in), (2, residual)])

            c = ve.alloc_register("dve_tp_count")
            c2 = ve.alloc_register("dve_tp_count2")
            cg = [ve.alloc_register(f"dve_tp_got{k}") for k in range(2)]
            ve.reg_mov(c, 1)
            ve.reg_mov(c2, 2)
            ve.reg_mov(cg[0], 16)
            ve.reg_mov(cg[1], 16)
            ve.wait_ge(G[1]["x1_stored"], 16 * NW)
            ve.wait_ge(G[1]["up_ready"], NW)
            ve.nop().then_inc(M["msg_ready"], 1)
            ve.nop().then_inc(M["u_used"], 1)
            ve.tensor_copy(iota_w[:, :], iota[:, :])

            def messages(w):
                lo, hi = window_range(ve, w, 1)
                ve.drain()
                with ve.Fori(lo, hi) as g:
                    n = ve.snap(c)
                    buf = (n % 2) * (4 * D)
                    s0 = ring[:, 0:2, 0:P]
                    ve.wait_ge(M["q0"], c2)
                    for k in range(2):
                        ve.scalar_tensor_tensor(out=q1[:, k, :], in0=ring[:, k, 2 * P:3 * P], scalar=yg[:, 4 * k + 2:4 * k + 3],
                                                in1=q0[:, k, :], op0=ALU.mult, op1=ALU.add)
                    ve.drain()
                    for k in range(2):
                        ve.scalar_tensor_tensor(out=q2[:, k, :], in0=ring[:, k, 3 * P:4 * P], scalar=yg[:, 4 * k + 3:4 * k + 4],
                                                in1=q1[:, k, :], op0=ALU.mult, op1=ALU.add)
                    ve.wait_ge(M["w_done"], n + 1)
                    for k in range(2):
                        ve.tensor_tensor(t2[:, k, :], w_bank[k][1][:, 0:P], ring[:, k, 0:P], ALU.mult)
                    ve.drain()
                    ve.nop().then_inc(M["t2"], 1)
                    ve.wait_ge(M["seg_done"], n)
                    for k in range(2):
                        ve.tensor_tensor(msg[:, bass.ds(buf + (k * 2 * D + D), P)], q2[:, k, :], w_bank[k][1][:, P:2 * P], ALU.mult)
                    ve.wait_ge(M["w13"], c2)
                    for k in range(2):
                        ve.tensor_tensor(msg[:, bass.ds(buf + k * 2 * D, P)], w13[:, k, 0:P], ring[:, k, 0:P], ALU.mult)
                        ve.tensor_tensor(msg[:, bass.ds(buf + (k * 2 * D + P), 3 * P)].rearrange("p (m u) -> p m u", m=3),
                                         w13[:, k, P:2 * P].unsqueeze(1).broadcast_to([P, 3, P]),
                                         ring[:, k, P:4 * P].rearrange("p (m u) -> p m u", m=3), ALU.mult)
                    ve.drain()
                    ve.nop().then_inc(M["u_used"], 1)
                    ve.wait_ge(M["p2"], n)
                    ve.nop().then_inc(M["msg_ready"], 1)
                    ve.wait_ge(M["seg_done"], n + 1)
                    ve.tensor_tensor(oh[:, 0:2, :], iota_w[:, :].unsqueeze(1).broadcast_to([P, 2, P]),
                                     dst_f[:, bass.ds(g * 2, 2)].unsqueeze(2).broadcast_to([P, 2, P]),
                                     ALU.is_equal).then_inc(M["onehot"], 1)
                    ve.reg_add(c, c, 1)
                    ve.reg_add(c2, c2, 2)
                ve.drain()
                ve.tensor_scalar(iota_w[:, :], iota_w[:, :], float(P), None, ALU.add)

            def keep_b(w):
                ve.wait_ge(M["sum_done"], w + 1)
                after(ve, M["turned"], w)
                ve.tensor_copy(mB[:, :], bank[1][:, :]).then_inc(M["mB"], 1)

            def copy_mT(w):
                ve.wait_ge(M["turned"], w + 1)
                after(ve, M["o_done"], w)
                ve.tensor_copy(mT[:, 4:8, :], m_bank[1][:, :].rearrange("p (c n) -> p c n", c=4)).then_inc(M["mT_b"], 1)

            def finish(w):
                ve.wait_ge(M["x1_in"], (w + 1) * 16)
                ve.wait_ge(M["o_done"], w + 1)
                after(ve, M["stored"], w, 16)
                ve.tensor_tensor(x1[:, 0:P], xw[:, 0:P], bank[6][:, 0:P], ALU.add)
                ve.tensor_tensor(x1[:, P:].rearrange("p (v m) -> p v m", m=3), xw[:, P:].rearrange("p (v m) -> p v m", m=3),
                                 bank[6][:, P:].rearrange("p (m v) -> p v m", m=3), ALU.add).then_inc(M["out_ready"], 1)

            peeled(ve, [(0, messages), (1, copy_mT), (0, keep_b), (1, finish)])

        @block.tensor
        def _(pe):
            pe.wait_ge(s_wsc, 1)

            def radial(j):
                for b in range(2):
                    pe.wait_ge(ef_in[b], j * 16 + 16)
                    pe.matmul(bank[0 + b][:, :], w1[:, :], ef[:, b, :], start=True, stop=True).then_inc(m1, 1)
                for b in range(2):
                    pe.wait_ge(a1, j * 2 + 1 + b)
                    pe.matmul(bank[2 + b][:, :], w2[:, :], hA[:, b, :], start=True, stop=True).then_inc(m2, 1)
                for b in range(2):
                    pe.wait_ge(a2, j * 2 + 1 + b)
                    if not isinstance(j, int):
                        pe.wait_ge(a3, j * 2 - 1 + b)
                    pe.matmul(bank[4 + b][:, :], w3[:, :], hB[:, b, :], start=True, stop=True).then_inc(m3, 1)

            looped(pe, radial, NG2 // 8)
            def touch(t, n, start):
                return pe.matmul(t, zeros[:, 0:P], zeros[:, 0:n], start=start, stop=not start, skip_group_check=True)

            touch(bank[6][:, 0:NW], NW, True)
            with pe.Fori(0, NT // 16) as j:
                for b in range(2):
                    pe.wait_ge(oh_rdy, j * 2 + 1 + b)
                    for t in range(8):
                        ins = pe.matmul(bank[6][:, 0:NW], ohl[:, b, t, :], ohh[:, b, t, :], start=False, stop=False,
                                        skip_group_check=True)
                    ins.then_inc(oh_used, 1)
            touch(bank[6][:, 0:NW], NW, False).then_inc(deg_sum, 1)
            pe.wait_ge(s_big, 16 * len(W))
            pe.wait_ge(a3, NG2 // 4)
            pe.wait_ge(s_rld, 16)

            for L in range(2):
                S = G[L]
                WC, WL = (W["W0"], W["lw0"]) if L == 0 else (W["W1"], W["lw1"])
                c = pe.alloc_register(f"pe_gcn{L}_count")
                cg = pe.alloc_register(f"pe_gcn{L}_got")
                pe.reg_mov(c, 1)
                pe.reg_mov(cg, 16)
                for k in range(4):
                    pe.nop().then_inc(S["used"][k], 1)

                def edge_sum(w, S=S, c=c, cg=cg):
                    lo, hi = window_range(pe, w, 0)
                    after(pe, S["agg_ready"], w)
                    touch(bank[0][:, :], D, True)
                    with pe.Fori(lo, hi) as g:
                        for k in range(4):
                            if k % 2 == 0:
                                pe.wait_ge(S["onehot_b" if k else "onehot_a"], c)
                            pe.wait_ge(S["got"][k], cg)
                            pe.matmul(bank[0][:, :], oh[:, k, :], ring[:, k, :], start=False, stop=False,
                                      skip_group_check=True).then_inc(S["used"][k], 1)
                        pe.reg_add(c, c, 1)
                        pe.reg_add(cg, cg, 16)
                    touch(bank[0][:, :], D, False).then_inc(S["sum_done"], 1)

                def turn(w, S=S):
                    pe.wait_ge(S["agg_ready"], w + 1)
                    after(pe, S["at_a"], w)
                    after(pe, S["at_b"], w)
                    for i in range(8):
                        sr = (agg if i < 4 else hw)[:, (i % 4) * P:(i % 4 + 1) * P]
                        ins = pe.transpose(bank[1 + i // 4][:, (i % 4) * P:(i % 4 + 1) * P], sr, ident[:, :])
                    ins.then_inc(S["turned"], 1)

                def dense(w, S=S, WC=WC, WL=WL):
                    pe.wait_ge(S["at_a"], w + 1)
                    pe.wait_ge(S["at_b"], w + 1)
                    after(pe, S["y_read"], w)
                    for i in range(8):
                        ins = pe.matmul(bank[3][:, :], AT[:, i, :], (WC if i < 4 else WL)[:, i % 4, :],
                                        start=(i == 0), stop=(i == 7))
                    ins.then_inc(S["dense_done"], 1)

                def turn_xs(w, S=S):
                    pe.wait_ge(S["xs_ready"], w + 1)
                    after(pe, S["xT_ready"], w)
                    for i in range(4):
                        ins = pe.transpose(bank[4][:, i * P:(i + 1) * P], xs[:, i * P:(i + 1) * P], ident[:, :])
                    ins.then_inc(S["xs_turned"], 1)

                def project(w, S=S):
                    pe.wait_ge(S["xT_ready"], w + 1)
                    after(pe, S["x1_ready"], w)
                    for i in range(4):
                        ins = pe.matmul(bank[5][:, :], xT[:, i, :], W["pw"][:, i, :], start=(i == 0), stop=(i == 3))
                    ins.then_inc(S["proj_done"], 1)

                def turn_h(w, S=S):
                    pe.wait_ge(S["h_ready"], w + 1)
                    after(pe, S["hT_ready"], w)
                    for i in range(4):
                        sr = hrel[:, 0, 0:P] if i == 0 else hrel[:, 0, P:].rearrange("p (u m) -> p m u", m=3)[:, i - 1, :]
                        ins = pe.transpose(bank[6][:, i * P:(i + 1) * P], sr, ident[:, :])
                    ins.then_inc(S["h_turned"], 1)

                def up(w, S=S):
                    pe.wait_ge(S["hT_ready"], w + 1)
                    after(pe, S["up_ready"], w)
                    for i in range(4):
                        ins = pe.matmul(bank[7][:, i * P:(i + 1) * P], hT[:, i, :], wup[:, min(i, 1), :], start=True, stop=True)
                    ins.then_inc(S["up_done"], 1)

                if L == 0:
                    peeled(pe, [(0, edge_sum), (1, turn), (1, dense), (2, lambda w: None)])
                else:
                    peeled(pe, [(0, edge_sum), (3, turn_h), (1, turn), (3, up), (1, dense), (2, turn_xs), (2, project)])

            c = pe.alloc_register("pe_tp_count")
            cp = pe.alloc_register("pe_tp_prev")
            ch = pe.alloc_register("pe_tp_hidden")
            pe.reg_mov(c, 1)
            pe.reg_mov(cp, 1)
            pe.reg_mov(ch, 16)
            pe.wait_ge(G[1]["up_ready"], NW)
            pe.wait_ge(G[1]["agg_ready"], NW)
            pe.wait_ge(G[1]["x1_ready"], NW)
            pe.nop().then_inc(M["w_done"], 1)
            pe.nop().then_inc(M["seg_done"], 1)
            pe.nop().then_inc(M["seg_done"], 1)

            def edge_weights():
                pe.wait_ge(M["hid_in"], ch)
                pe.reg_add(ch, ch, 16)
                pe.wait_ge(M["msg_ready"], c)
                pe.reg_add(c, c, 1)
                for k in range(2):
                    for h in range(2):
                        ins = pe.matmul(w_bank[k][h][:, 0:2 * P], hid[k * HID:(k + 1) * HID, :],
                                        w4[k * HID:(k + 1) * HID, h * 2 * P:(h + 1) * 2 * P], start=True, stop=True)
                ins.then_inc(M["w_done"], 1)

            def sum_pair():
                n = pe.snap(cp)
                pe.wait_ge(M["msg_ready"], n + 1)
                pe.wait_ge(M["onehot"], n)
                for k in range(2):
                    for h in range(2):
                        ins = pe.matmul(bank[h][:, :], oh[:, k, :], msg[:, bass.ds((n % 2) * (4 * D) + (k * 2 + h) * D, D)],
                                        start=False, stop=False, skip_group_check=True)
                ins.then_inc(M["seg_done"], 1)
                pe.reg_add(cp, cp, 1)

            def pair_sums(w):
                lo, hi = window_range(pe, w, 1)
                after(pe, M["mA"], w)
                after(pe, M["mB"], w)
                touch(bank[0][:, :], D, True)
                touch(bank[1][:, :], D, True)
                edge_weights()
                with pe.Fori(lo + 1, hi) as g:
                    edge_weights()
                    sum_pair()
                sum_pair()
                touch(bank[0][:, :], D, False)
                touch(bank[1][:, :], D, False).then_inc(M["sum_done"], 1)

            def turn_m(w):
                pe.wait_ge(M["mA"], w + 1)
                pe.wait_ge(M["mB"], w + 1)
                after(pe, M["mT_a"], w)
                after(pe, M["mT_b"], w)
                after(pe, M["out_ready"], w)
                for i in range(8):
                    sr = (mA if i < 4 else mB)[:, (i % 4) * P:(i % 4 + 1) * P]
                    ins = pe.transpose(m_bank[i // 4][:, (i % 4) * P:(i % 4 + 1) * P], sr, ident[:, :])
                ins.then_inc(M["turned"], 1)

            def out_product(w):
                pe.wait_ge(M["mT_a"], w + 1)
                pe.wait_ge(M["mT_b"], w + 1)
                after(pe, M["out_ready"], w)
                for i in range(4):
                    first, second = (0, 4) if i == 0 else (4 + i, i)
                    o = bank[6][:, i * P:(i + 1) * P]
                    pe.matmul(o, mT[:, first, :], wo[:, 0 if i == 0 else 2, :], start=True, stop=False)
                    ins = pe.matmul(o, mT[:, second, :], wo[:, 1 if i == 0 else 3, :], start=False, stop=True)
                ins.then_inc(M["o_done"], 1)

            peeled(pe, [(0, pair_sums), (1, turn_m), (1, out_product)])


_SHORT = {"W0": "L0_gnn_W0", "b0": "L0_gnn_b0", "lb0": "L0_gnn_lb0", "g0": "L0_gnn_g0", "be0": "L0_gnn_be0",
          "W1": "L0_gnn_W1", "b1": "L0_gnn_b1", "lb1": "L0_gnn_lb1", "g1": "L0_gnn_g1", "be1": "L0_gnn_be1",
          "pb": "L0_gnn_pb", "W_up0": "L1_gnn_W_up0", "W_up1": "L1_gnn_W_up1", "W_mlp1": "L1_gnn_W_mlp1",
          "W_mlp2": "L1_gnn_W_mlp2", "W_mlp3": "L1_gnn_W_mlp3", "W_mlp4": "L1_gnn_W_mlp4",
          "W_out0": "L1_gnn_W_out0", "W_out1": "L1_gnn_W_out1", "x": "x"}


def kernel(**inputs):
    import numpy as _np
    import concourse.bacc as _bacc
    from concourse import mybir as _mybir
    from concourse.bass_utils import run_bass_kernel_spmd as _run

    nc = _bacc.Bacc("TRN2", target_bir_lowering=False, num_devices=1)
    laid = {k: _np.asarray(inputs[v]) for k, v in _SHORT.items()}
    for k, v in (("lw0", "L0_gnn_lw0"), ("lw1", "L0_gnn_lw1"), ("pw", "L0_gnn_pw")):
        laid[k] = _np.asarray(inputs[v]).T
    pad = NT * P - E
    src, dst = _np.asarray(inputs["src"]), _np.asarray(inputs["dst"])
    ea, ef = _np.asarray(inputs["edge_attr_4"]), _np.asarray(inputs["edge_attr_8"])
    laid["src_t"] = _np.pad(src, (0, pad)).reshape(NT, P).T
    laid["dst_t"] = _np.pad(dst, (0, pad), constant_values=-1).reshape(NT, P).T
    laid["dst_g"] = _np.pad(dst, (0, pad), mode="edge").reshape(NG2 // 4, 4 * 256)
    laid["ea_t"] = _np.pad(ea, ((0, pad), (0, 0))).reshape(NT, P, 4).transpose(1, 0, 2).reshape(P, NT * 4)
    laid["ef_t"] = (_np.pad(ef, ((0, pad), (0, 0))).reshape(NG2, 2, P, RB).transpose(1, 3, 0, 2)
                    .reshape(2 * RB, NG2 * P))
    arrays, args = {}, {}
    for name, v in laid.items():
        v = _np.ascontiguousarray(v)
        arrays[f"in_{name}_dram"] = v
        args[name] = nc.dram_tensor(f"in_{name}_dram", v.shape, _mybir.dt.from_np(v.dtype), kind="ExternalInput").ap()
    out = nc.dram_tensor("out_0_dram", (N, D), _mybir.dt.float32, kind="ExternalOutput").ap()
    build(nc, args, out)
    r = _run(nc, [arrays], core_ids=[0])
    return r.results[0]["out_0_dram"]
```

```python
from contextlib import ExitStack

import concourse.bass as bass
from concourse import mybir

P = 128
N, D, E = 6250, 512, 100000
NW = (N + P - 1) // P
NPAD = NW * P
TAIL = N - (NW - 1) * P
NT = 784
NG = NT // 2
NB = 8
KC = D // P
HID = 64
RB = 8
EPS = 1e-5
SILU_2MOM = 1.679177
AVG = 10.0

ALU = mybir.AluOpType
ACT = mybir.ActivationFunctionType
F32 = mybir.dt.float32
BF16 = mybir.dt.bfloat16
F16 = mybir.dt.float16
I32 = mybir.dt.int32
X = mybir.AxisListType.X


def build(nc, a, out):
    with ExitStack() as ctx:
        def sb(name, shape, dt=F32):
            return ctx.enter_context(nc.sbuf_tensor(name, shape, dt))

        def sem(name):
            return ctx.enter_context(nc.semaphore(name))

        def dram(name, shape, dt=F32):
            return nc.dram_tensor(name, shape, dt).ap()

        hid_d = dram("hid_d", (NG, P, P))
        tab_d = [dram("tab0_d", (NPAD, 2 * D), F16), dram("tab1_d", (NPAD, 2 * D), F16)]
        r0_d = dram("r0_d", (NPAD, D))
        x1_d = dram("x1_d", (NPAD, D))
        up_d = dram("up_d", (NPAD, D))
        ext_d = dram("ext_d", (2, NG))
        rng_d = dram("rng_d", (NW, 2), I32)

        bank = [ctx.enter_context(nc.psum_tensor(f"bank{i}", [P, D], F32)) for i in range(8)]

        src_i = sb("src_i", [P, NT], I32)
        dst_f = sb("dst_f", [P, NT])
        y_t = sb("y_t", [P, NT * 4])
        ident = sb("ident", [P, P])
        iota = sb("iota", [P, P])
        iota_w = sb("iota_w", [P, P])
        zeros = sb("zeros", [P, D], BF16)
        eps = sb("eps", [P, 1])
        rdeg = sb("rdeg", [P, NW])
        dinv = sb("dinv", [P, NW])
        rng = sb("rng", [1, 2 * NW], I32)
        identh = sb("identh", [P, P], F16)
        dup = sb("dup", [P, 2, NW])
        dse = sb("dse", [P, 2, NW])
        rse = sb("rse", [P, 2, NW])
        bound = sb("bound", [P, 2, 8])
        dense_w = sb("dense_w", [P, 5, KC, D])
        W = {k: dense_w[:, i, :, :] for i, k in enumerate(("W0", "lw0", "W1", "lw1", "pw"))}
        wup = sb("wup", [P, 2, P])
        w1 = sb("w1", [2 * RB, P])
        w2 = sb("w2", [P, P])
        w3 = sb("w3", [P, P])
        w4 = sb("w4", [P, D])
        wo = sb("wo", [P, 4, P])
        bia = {k: sb("v_" + k, [P, D]) for k in ("b0", "lb0", "g0", "be0", "b1", "lb1", "g1", "be1", "pb")}

        ring = sb("ring", [P, NB * 2 * D])
        ring_h = ring[:, :].bitcast(F16).rearrange("p (b k n) -> p b k n", b=NB, k=2)
        ring_u = ring[:, 0:4 * D].rearrange("p (b k n) -> p b k n", b=2, k=2)
        early = [ring[:, i * NT:(i + 1) * NT] for i in range(5)]
        dst_i, hi_i, lo_i = (t.bitcast(I32) for t in early[0:3])
        hi_f, lo_f = early[3:5]
        dst_g = ring[0:NG // 4, 5 * NT:5 * NT + 1024].bitcast(I32)
        ohl = sb("ohl", [P, 2, 8, P], BF16)
        ohh = sb("ohh", [P, 2, 8, NW], BF16)
        ext = sb("ext", [NG // 4, 2, 4])
        extb = sb("extb", [NW, 2, NG])
        asc = sb("asc", [NW, NG])
        asc_i = sb("asc_i", [NW, NG], I32)
        rtmp = sb("rtmp", [NW, NG])
        rtmp2 = sb("rtmp2", [NW, NG])
        wlo = sb("wlo", [NW, 1])
        wlo_i = sb("wlo_i", [NW, 1], I32)
        rcol = sb("rcol", [NW, 8])
        rcol_i = sb("rcol_i", [NW, 2], I32)
        iota_i = sb("iota_i", [P, P], I32)
        pid_i = sb("pid_i", [P, 1], I32)
        pid = sb("pid", [P, 1])
        ef = sb("ef", [2 * RB, 2, D])
        hA = sb("hA", [P, 2, D])
        hB = sb("hB", [P, 2, D])
        hC = sb("hC", [P, 2, D])

        xin = sb("xin", [P, 2, D])
        hrel = sb("hrel", [P, 2, D])
        tn = sb("tn", [P, 2, D])
        t32 = sb("t32", [P, 2, D])
        tout = sb("tout", [P, 2, 2 * D], F16)
        st = sb("st", [P, 2, 6])
        mv = sb("mv", [P, 2, 8])

        ohp = sb("ohp", [P, NB, 2, P], F16)
        oh = sb("oh", [P, 2, 2, P])
        idx = sb("idx", [P, NB, 2], I32)
        tw = sb("tw", [P, 2 * D], F16)
        hw0 = hA[:, 0, :]
        hw = sb("hw", [P, D])
        agg = sb("agg", [P, D])
        AT = sb("AT", [P, 8, P])
        yb = sb("yb", [P, D])
        r = sb("r", [P, D])
        r0w = sb("r0w", [P, D])
        xs = sb("xs", [P, D])
        xT = sb("xT", [P, KC, P])
        xw = sb("xw", [P, D])
        x1 = sb("x1", [P, D])
        hT = sb("hT", [P, KC, P])
        uo = sb("uo", [P, D])

        msg = dense_w[:, 0:2, :, :].rearrange("p a (k h) n -> p a k h n", k=2)
        hid = hC[:, 0, 0:256].rearrange("p (b n) -> p b n", b=2)
        yg = hC[:, 1, 0:16].rearrange("p (b n) -> p b n", b=2)
        w13 = hA[:, 0, :].rearrange("p (k n) -> p k n", k=2)
        t2, q1 = (hA[:, 1, i * 256:(i + 1) * 256].rearrange("p (k n) -> p k n", k=2) for i in range(2))
        q2 = hB[:, 0, 0:256].rearrange("p (k n) -> p k n", k=2)
        q0 = hB[:, 1, :].rearrange("p (b k n) -> p b k n", b=2, k=2)
        mA, mB, mT = agg, hw, AT

        def s(name):
            return sem(name)

        s_edge, s_small, s_big = s("edges_in"), s("small_weights_in"), s("big_weights_in")
        s_gext, s_extst, s_extld, s_rst, s_rld = (s("ext_ready"), s("ext_stored"), s("ext_loaded"),
                                                  s("ranges_stored"), s("ranges_loaded"))
        s_cst, s_wz, s_wsc, s_rcol = s("constants_ready"), s("weights_zeroed"), s("weights_scaled"), s("ranges_ready")
        ef_in = [s(f"ef_in{i}") for i in range(2)]
        hid_out = [s(f"hid_out{i}") for i in range(2)]
        m1, m2, m3 = s("radial1_sum"), s("radial2_sum"), s("radial3_sum")
        a1, a2, a3 = s("radial1_act"), s("radial2_act"), s("radial3_act")
        oh_rdy, oh_used = s("degree_onehot_ready"), s("degree_onehot_used")
        deg_sum, deg_ready, deg_sq = s("degree_summed"), s("dinv_ready"), s("degree_root")
        x_in = [s(f"x_in{i}") for i in range(2)]
        t_st = [s(f"table0_stored{i}") for i in range(2)]
        n_st1, n_sd1, n_rs1, n_h, n_st2, n_sd2, n_rs2, n_t, n_out = (
            s("norm_stats1"), s("norm_std1"), s("norm_scale1"), s("norm_relu"), s("norm_stats2"),
            s("norm_std2"), s("norm_scale2"), s("norm_table_scaled"), s("norm_table_ready"))
        n_g, n_t32, n_hi = s("norm_times_g"), s("norm_table_f32"), s("norm_table_high")

        def peeled(eng, stages):
            depth = max(d for d, _ in stages)
            for w in range(depth + 1):
                for d, f in stages:
                    if w - d >= 0:
                        f(w - d)
            with eng.Fori(depth + 1, NW) as w:
                for d, f in stages:
                    f(w - d)
            for w in range(NW, NW + depth):
                for d, f in stages:
                    if w - d < NW:
                        f(w - d)

        def after(eng, sm, w, per=1):
            if isinstance(w, int):
                if w > 0:
                    eng.wait_ge(sm, w * per)
            else:
                eng.wait_ge(sm, w * per)

        def looped(eng, body, n):
            body(0)
            with eng.Fori(1, n) as i:
                body(i)

        def rows(t, w):
            return t[w * P:(w + 1) * P, :] if isinstance(w, int) else t[bass.ds(w * P, P), :]

        def col(t, w):
            return t[:, w:w + 1] if isinstance(w, int) else t[:, bass.ds(w, 1)]

        def window_range(eng, w):
            at = w * 2
            if isinstance(w, int):
                la, ha = rng[0:1, at:at + 1], rng[0:1, at + 1:at + 2]
            else:
                la, ha = rng[0:1, bass.ds(at, 1)], rng[0:1, bass.ds(w * 2 + 1, 1)]
            return eng.value_load(la, min_val=0, max_val=NG - 2), eng.value_load(ha, min_val=2, max_val=NG)

        def pick(eng, sel, lo, hi, body):
            if hi - lo == 1:
                body(lo)
                return
            mid = (lo + hi) // 2
            with eng.If(sel < mid):
                pick(eng, sel, lo, mid, body)
            with eng.Else():
                pick(eng, sel, mid, hi, body)

        block = ctx.enter_context(nc.Block())

        def gcn_sems(L):
            names = ("idx_ready", "used", "onehot", "sum_done", "agg_ready", "self_in", "self_high", "self_done",
                     "turned", "at_a", "at_b", "dense_done", "y_read", "relu_done", "r_stored", "tab_stored",
                     "stats", "std", "scale", "tn", "t32", "high", "tout", "r0_in", "xs_ready", "xs_turned", "xT_ready",
                     "proj_done", "x_in", "x1_ready", "x1_stored", "h_ready", "h_turned", "hT_ready", "up_done",
                     "up_ready", "up_stored")
            S = {k: s(f"gcn{L}_{k}") for k in names}
            S["got"] = [s(f"gcn{L}_gathered{k}") for k in range(NB)]
            return S

        G = [gcn_sems(0), gcn_sems(1)]
        w_bank = [[bank[2], bank[3]], [bank[7], bank[5]]]
        m_bank = [bank[4], bank[6]]
        M = {k: s("tp_" + k) for k in (
            "idx_ready", "w_done", "w13", "t2", "q0", "p2", "u_used", "msg_ready", "onehot", "seg_done",
            "sum_done", "mA", "mB", "turned", "mT_a", "mT_b", "o_done", "x1_in", "out_ready", "stored")}
        M["got"] = [s(f"tp_gathered{k}") for k in range(2)]
        M["hid_in"] = [s(f"tp_hidden_in{k}") for k in range(2)]

        @block.sync
        def _(sp):
            for t, k in ((src_i[:, :], "src_t"), (dst_i, "dst_t"), (dst_g, "dst_g"), (y_t[:, :], "ea_t")):
                sp.dma_start(t, a[k]).then_inc(s_edge, 16)
            for k in bia:
                sp.dma_start(bia[k][:, :], a[k].rearrange("(a d) -> a d", a=1).broadcast_to([P, D])).then_inc(s_small, 16)
            sp.dma_start(wup[:, 0, :], a["W_up0"]).then_inc(s_small, 16)
            sp.dma_start(wup[:, 1, :], a["W_up1"]).then_inc(s_small, 16)
            sp.dma_start(wo[:, 0:2, :], a["W_out0"].rearrange("(c p) n -> p c n", p=P)).then_inc(s_small, 16)
            sp.dma_start(wo[:, 2:4, :], a["W_out1"].rearrange("(c p) n -> p c n", p=P)).then_inc(s_small, 16)
            sp.wait_ge(s_wz, 3)
            for t, k, n in ((w1, "W_mlp1", RB), (w2, "W_mlp2", HID), (w3, "W_mlp3", HID)):
                for h in range(2):
                    sp.dma_start(t[h * n:(h + 1) * n, h * HID:(h + 1) * HID], a[k]).then_inc(s_small, 16)
            for h in range(2):
                for c, f in enumerate((0, 2, 1, 3)):
                    sp.dma_start(w4[h * HID:(h + 1) * HID, c * P:(c + 1) * P],
                                 a["W_mlp4"][:, f * P:(f + 1) * P]).then_inc(s_small, 16)
            sp.wait_ge(s_gext, 1)
            sp.dma_start(ext_d.rearrange("a (p q) -> p a q", q=4), ext[:, :, :]).then_inc(s_extst, 16)
            for k in W:
                sp.dma_start(W[k][:, :, :], a[k].rearrange("(c p) n -> p c n", p=P)).then_inc(s_big, 16)
            sp.wait_ge(s_extst, 16)
            sp.dma_start(extb[:, :, :], ext_d.rearrange("(o a) g -> o a g", o=1).broadcast_to([NW, 2, NG])).then_inc(s_extld, 16)
            sp.wait_ge(s_rcol, 1)
            sp.dma_start(rng_d, rcol_i[:, :]).then_inc(s_rst, 16)
            sp.wait_ge(s_rst, 16)
            sp.dma_start(rng[:, :], rng_d.rearrange("(o w) k -> o (w k)", o=1)).then_inc(s_rld, 16)

            sp.wait_ge(s_wsc, 1)
            def load_ef(j):
                for b in range(2):
                    if not isinstance(j, int) or j > 0:
                        sp.wait_ge(m1, j * 2 - 1 + b)
                    sp.dma_start(ef[:, b, :], a["ef_t"][:, bass.ds((j * 2 + b) * D, D)]).then_inc(ef_in[b], 16)

            def store_hid(j):
                for b in range(2):
                    sp.wait_ge(a3, j * 2 + 1 + b)
                    sp.dma_start(hid_d[bass.ds((j * 2 + b) * 4, 4), :, :].rearrange("g p e -> p g e"),
                                 hC[:, b, :].rearrange("p (g e) -> p g e", g=4)).then_inc(hid_out[b], 16)

            load_ef(0)
            with sp.Fori(0, NG // 8 - 1) as j:
                load_ef(j + 1)
                store_hid(j)
            store_hid(NG // 8 - 1)

            def load_x(j):
                for b in range(2):
                    if not isinstance(j, int) or j > 0:
                        sp.wait_ge(n_h, j * 2 - 1 + b)
                    sp.dma_start(xin[:, b, :], a["x"][bass.ds((j * 2 + b) * P, P), :]).then_inc(x_in[b], 16)

            def store_table(j):
                for b in range(2):
                    sp.wait_ge(n_out, j * 2 + 1 + b)
                    sp.dma_start(tab_d[0][bass.ds((j * 2 + b) * P, P), :], tout[:, b, :]).then_inc(t_st[b], 16)

            load_x(0)
            with sp.Fori(0, NW // 2 - 1) as j:
                load_x(j + 1)
                store_table(j)
            sp.wait_ge(n_h, NW - 2)
            sp.dma_start(xin[0:TAIL, 0, :], a["x"][N - TAIL:N, :]).then_inc(x_in[0], 16)
            store_table(NW // 2 - 1)
            sp.wait_ge(n_out, NW)
            sp.dma_start(tab_d[0][(NW - 1) * P:, :], tout[:, 0, :]).then_inc(t_st[0], 16)
            sp.wait_ge(t_st[0], 16 * (NW // 2 + 1))
            sp.wait_ge(t_st[1], 16 * (NW // 2))

            for L in range(2):
                S = G[L]

                def self_rows(w, S=S, L=L):
                    after(sp, S["self_done"], w)
                    after(sp, S["sum_done"], w)
                    sp.dma_start(tw[:, :], rows(tab_d[L], w)).then_inc(S["self_in"], 16)

                def store_r(w, S=S):
                    sp.wait_ge(S["relu_done"], w + 1)
                    sp.dma_start(rows(r0_d, w), r[:, :]).then_inc(S["r_stored"], 16)

                def store_tab(w, S=S):
                    sp.wait_ge(S["tout"], w + 1)
                    sp.dma_start(rows(tab_d[1], w), tout[:, 0, :]).then_inc(S["tab_stored"], 16)

                def load_r0(w, S=S):
                    after(sp, S["xs_ready"], w)
                    sp.dma_start(r0w[:, :], rows(r0_d, w)).then_inc(S["r0_in"], 16)

                def load_x(w, S=S):
                    after(sp, S["x1_ready"], w)
                    if isinstance(w, int) and w == NW - 1:
                        sp.dma_start(xw[0:TAIL, :], a["x"][N - TAIL:N, :]).then_inc(S["x_in"], 16)
                    else:
                        sp.dma_start(xw[:, :], rows(a["x"], w)).then_inc(S["x_in"], 16)

                def store_x1(w, S=S):
                    sp.wait_ge(S["x1_ready"], w + 1)
                    sp.dma_start(rows(x1_d, w), x1[:, :]).then_inc(S["x1_stored"], 16)

                def store_up(w, S=S):
                    sp.wait_ge(S["up_ready"], w + 1)
                    sp.dma_start(rows(up_d, w), uo[:, :]).then_inc(S["up_stored"], 16)

                if L == 0:
                    peeled(sp, [(0, self_rows), (2, store_r), (2, store_tab)])
                    sp.wait_ge(S["r_stored"], 16 * NW)
                    sp.wait_ge(S["tab_stored"], 16 * NW)
                else:
                    peeled(sp, [(0, self_rows), (2, load_r0), (2, load_x), (3, store_up), (2, store_x1)])
                    sp.wait_ge(S["x1_stored"], 16 * NW)
                    sp.wait_ge(S["up_stored"], 16 * NW)

            sp.wait_ge(hid_out[0], 16 * (NG // 8))
            sp.wait_ge(hid_out[1], 16 * (NG // 8))
            c = sp.alloc_register("sp_tp_count")
            sp.reg_mov(c, 1)

            def hidden(w):
                lo, hi = window_range(sp, w)
                with sp.Fori(lo, hi) as g:
                    n = sp.snap(c)

                    def load(b):
                        sp.wait_ge(M["w_done"], n)
                        sp.reg_add(c, c, 1)
                        sp.dma_start(hid[:, b, :], hid_d[bass.ds(g, 1), :, :].rearrange("g p e -> p (g e)")).then_inc(
                            M["hid_in"][b], 16)
                    pick(sp, sp.snap(n % 2), 0, 2, load)

            def load_x1(w):
                after(sp, M["out_ready"], w)
                sp.dma_start(xw[:, :], rows(x1_d, w)).then_inc(M["x1_in"], 16)

            def store_out(w):
                sp.wait_ge(M["out_ready"], w + 1)
                if isinstance(w, int) and w == NW - 1:
                    sp.dma_start(out[N - TAIL:N, :], x1[0:TAIL, :]).then_inc(M["stored"], 16)
                else:
                    sp.dma_start(rows(out, w), x1[:, :]).then_inc(M["stored"], 16)

            peeled(sp, [(0, hidden), (2, store_out), (1, load_x1)])
            sp.wait_ge(M["stored"], 16 * NW)

        @block.gpsimd
        def _(g_):
            g_.iota(iota_i[:, :], [[1, P]], base=0, channel_multiplier=0).then_inc(s_cst, 1)
            g_.iota(pid_i[:, :], [[1, 1]], base=0, channel_multiplier=1).then_inc(s_cst, 1)
            g_.iota(asc_i[:, :], [[1, NG]], base=1, channel_multiplier=0).then_inc(s_cst, 1)
            g_.iota(wlo_i[:, :], [[1, 1]], base=0, channel_multiplier=P).then_inc(s_cst, 1)
            g_.memset(eps[:, :], EPS).then_inc(s_cst, 1)
            g_.memset(zeros[:, :], 0.0).then_inc(s_cst, 1)
            g_.memset(w1[:, :], 0.0).then_inc(s_wz, 1)
            g_.memset(w2[:, :], 0.0).then_inc(s_wz, 1)
            g_.memset(w3[:, :], 0.0).then_inc(s_wz, 1)

            def norm_tiles(j, bs):
                for b in bs:
                    g_.wait_ge(n_t, j * 2 + 1 + b)
                    g_.tensor_tensor(tn[:, b, :], tn[:, b, :], bia["g0"][:, :], ALU.mult).then_inc(n_g, 1)
                for b in bs:
                    g_.wait_ge(n_hi, j * 2 + 1 + b)
                    g_.tensor_tensor(tout[:, b, D:], t32[:, b, :], tout[:, b, 0:D], ALU.subtract).then_inc(n_out, 1)

            looped(g_, lambda j: norm_tiles(j, (0, 1)), NW // 2)
            norm_tiles(NW // 2, (0,))

            def gathers(S, table, name, buffers, used, ring_v, idx_t):
                c = g_.alloc_register(f"pool_{name}_count")
                g_.reg_mov(c, 1)

                def body(w):
                    lo, hi = window_range(g_, w)
                    with g_.Fori(lo, hi) as g:
                        n = g_.snap(c)
                        g_.wait_ge(used, n)

                        def gather(b):
                            g_.tensor_copy(idx_t[:, b, :], src_i[:, bass.ds(g * 2, 2)]).then_inc(S["idx_ready"], 1)
                            g_.wait_ge(S["idx_ready"], c)
                            g_.reg_add(c, c, 1)
                            for k in range(2):
                                g_.indirect_dma_start(ring_v[:, b, k, :], None, table,
                                                      bass.IndirectOffsetOnAxis(idx_t[:, b, k:k + 1], 0)).then_inc(S["got"][b], 16)
                        pick(g_, g_.snap(n % buffers), 0, buffers, gather)
                peeled(g_, [(0, body)])

            g_.wait_ge(s_edge, 64)
            g_.wait_ge(s_rld, 16)
            g_.wait_ge(t_st[0], 16 * (NW // 2 + 1))
            g_.wait_ge(t_st[1], 16 * (NW // 2))
            gathers(G[0], tab_d[0], "gcn0", NB, G[0]["used"], ring_h, idx)
            g_.wait_ge(G[0]["tab_stored"], 16 * NW)
            gathers(G[1], tab_d[1], "gcn1", NB, G[1]["used"], ring_h, idx)
            g_.wait_ge(G[1]["up_stored"], 16 * NW)
            gathers(M, up_d, "tp", 2, M["u_used"], ring_u, idx)

        @block.scalar
        def _(ac):
            ac.wait_ge(s_small, 16 * (len(bia) + 4 + 6 + 8))
            ac.mul(w1[:, :], w1[:, :], RB ** -0.5)
            for t in (w2, w3):
                ac.mul(t[:, :], t[:, :], SILU_2MOM * HID ** -0.5)
            ac.mul(w4[:, 0:3 * P], w4[:, 0:3 * P], SILU_2MOM * HID ** -0.5)
            ac.mul(w4[:, 3 * P:], w4[:, 3 * P:], SILU_2MOM * HID ** -0.5 * 3 ** -0.5)
            ac.mul(wup[:, :, :], wup[:, :, :], P ** -0.5)
            ac.mul(wo[:, :, :], wo[:, :, :], (2 * P) ** -0.5 / AVG)
            ac.drain()
            ac.nop().then_inc(s_wsc, 1)
            def radial(j):
                for b in range(2):
                    ac.wait_ge(m1, j * 2 + 1 + b)
                    ac.activation(hA[:, b, :], bank[0 + b][:, :], ACT.Silu).then_inc(a1, 1)
                for b in range(2):
                    ac.wait_ge(m2, j * 2 + 1 + b)
                    ac.activation(hB[:, b, :], bank[2 + b][:, :], ACT.Silu).then_inc(a2, 1)
                for b in range(2):
                    after(ac, hid_out[b], j, 16)
                    ac.wait_ge(m3, j * 2 + 1 + b)
                    ac.activation(hC[:, b, :], bank[4 + b][:, :], ACT.Silu).then_inc(a3, 1)

            looped(ac, radial, NG // 8)
            ac.wait_ge(deg_ready, 1)
            ac.activation(rdeg[:, :], rdeg[:, :], ACT.Sqrt).then_inc(deg_sq, 1)

            def norm_tiles(base, j, bs):
                for b in bs:
                    ac.wait_ge(n_st1, base + 1 + b)
                    ac.activation(mv[:, b, 2:3], mv[:, b, 1:2], ACT.Sqrt, bias=eps[:, 0:1]).then_inc(n_sd1, 1)
                for b in bs:
                    ac.wait_ge(n_rs1, base + 1 + b)
                    ac.activation(hrel[:, b, :], xin[:, b, :], ACT.Relu, bias=mv[:, b, 4:5],
                                  scale=mv[:, b, 3:4]).then_inc(n_h, 1)
                for b in bs:
                    ac.wait_ge(n_st2, base + 1 + b)
                    ac.activation(mv[:, b, 2:3], mv[:, b, 1:2], ACT.Sqrt, bias=eps[:, 0:1]).then_inc(n_sd2, 1)
                for b in bs:
                    ac.wait_ge(n_rs2, base + 1 + b)
                    ac.activation(tn[:, b, :], hrel[:, b, :], ACT.Identity, bias=mv[:, b, 4:5],
                                  scale=mv[:, b, 3:4]).then_inc(n_t, 1)
                for b in bs:
                    ac.wait_ge(n_t32, base + 1 + b)
                    after(ac, t_st[b], j, 16)
                    ac.copy(tout[:, b, 0:D], t32[:, b, :]).then_inc(n_hi, 1)

            looped(ac, lambda j: norm_tiles(j * 2, j, (0, 1)), NW // 2)
            norm_tiles(NW - 1, NW // 2, (0,))
            ac.wait_ge(s_rld, 16)

            for L in range(2):
                S = G[L]

                def self_high(w, S=S, L=L):
                    ac.wait_ge(S["self_in"], (w + 1) * 16)
                    after(ac, S["self_done"], w)
                    ac.mul(hw0[:, :], tw[:, 0:D], col(rse[:, L, :], w)).then_inc(S["self_high"], 1)

                def aggregate(w, S=S, L=L):
                    ac.wait_ge(S["sum_done"], w + 1)
                    after(ac, S["turned"], w)
                    ac.mul(agg[:, :], bank[0][:, :], col(dse[:, L, :], w)).then_inc(S["agg_ready"], 1)

                def copy_at(w, S=S):
                    ac.wait_ge(S["turned"], w + 1)
                    after(ac, S["dense_done"], w)
                    ac.copy(AT[:, 0:4, :], bank[1][:, :].rearrange("p (c n) -> p c n", c=4)).then_inc(S["at_a"], 1)

                def relu_r(w, S=S, L=L):
                    ac.wait_ge(S["y_read"], w + 1)
                    if L == 0:
                        after(ac, S["r_stored"], w, 16)
                    else:
                        after(ac, S["xs_ready"], w)
                    ac.activation(r[:, :], yb[:, :], ACT.Relu).then_inc(S["relu_done"], 1)

                def std(w, S=S):
                    ac.wait_ge(S["stats"], w + 1)
                    ac.activation(mv[:, 0, 2:3], mv[:, 0, 1:2], ACT.Sqrt, bias=eps[:, 0:1]).then_inc(S["std"], 1)

                def scaled(w, S=S):
                    ac.wait_ge(S["scale"], w + 1)
                    ac.activation(tn[:, 0, :], r[:, :], ACT.Identity, bias=mv[:, 0, 4:5],
                                  scale=mv[:, 0, 3:4]).then_inc(S["tn"], 1)

                def high(w, S=S):
                    ac.wait_ge(S["t32"], w + 1)
                    after(ac, S["tab_stored"], w, 16)
                    ac.copy(tout[:, 0, 0:D], t32[:, 0, :]).then_inc(S["high"], 1)

                def copy_xT(w, S=S):
                    ac.wait_ge(S["xs_turned"], w + 1)
                    after(ac, S["proj_done"], w)
                    ac.copy(xT[:, :, :], bank[4][:, :].rearrange("p (c n) -> p c n", c=4)).then_inc(S["xT_ready"], 1)

                def relu_h(w, S=S):
                    ac.wait_ge(S["scale"], w + 1)
                    after(ac, S["h_turned"], w)
                    ac.activation(hrel[:, 0, :], x1[:, :], ACT.Relu, bias=mv[:, 0, 4:5],
                                  scale=mv[:, 0, 3:4]).then_inc(S["h_ready"], 1)

                def copy_hT(w, S=S):
                    ac.wait_ge(S["h_turned"], w + 1)
                    after(ac, S["up_done"], w)
                    ac.copy(hT[:, :, :], bank[6][:, :].rearrange("p (c n) -> p c n", c=4)).then_inc(S["hT_ready"], 1)

                def up_out(w, S=S):
                    ac.wait_ge(S["up_done"], w + 1)
                    after(ac, S["up_stored"], w, 16)
                    ac.copy(uo[:, :], bank[7][:, :]).then_inc(S["up_ready"], 1)

                if L == 0:
                    peeled(ac, [(0, self_high), (1, copy_at), (0, aggregate), (2, relu_r), (2, std), (2, scaled), (2, high)])
                else:
                    peeled(ac, [(0, self_high), (3, copy_hT), (1, copy_at), (0, aggregate), (3, up_out), (2, relu_r),
                                (2, copy_xT), (2, std), (2, relu_h)])

            c = ac.alloc_register("act_tp_count")
            ac.reg_mov(c, 1)

            def weigh(w):
                lo, hi = window_range(ac, w)
                with ac.Fori(lo, hi) as g:
                    n = ac.snap(c)

                    def pair(b):
                        ac.wait_ge(M["msg_ready"], n)
                        ac.copy(yg[:, b, :], y_t[:, bass.ds(g * 8, 8)])
                        ac.drain()
                        ac.wait_ge(M["got"][b], ac.snap((n + 1) // 2 * 32))
                        for k in range(2):
                            ins = ac.mul(q0[:, b, k, :], ring_u[:, b, k, P:2 * P], yg[:, b, 4 * k + 1:4 * k + 2])
                        ins.then_inc(M["q0"], 1)
                        ac.wait_ge(M["w_done"], n + 2)
                        for k in range(2):
                            ins = ac.mul(w13[:, k, :], w_bank[k][0][:, 0:2 * P], yg[:, b, 4 * k:4 * k + 1])
                        ins.then_inc(M["w13"], 1)
                        ac.wait_ge(M["t2"], n)
                        ac.wait_ge(M["seg_done"], n)
                        for k in range(2):
                            for m in range(3):
                                ins = ac.mul(msg[:, b, k, 1, P + m * P:2 * P + m * P], t2[:, k, :],
                                             yg[:, b, 4 * k + 1 + m:4 * k + 2 + m])
                        ins.then_inc(M["p2"], 1)
                        ac.reg_add(c, c, 1)
                    pick(ac, ac.snap(n % 2), 0, 2, pair)

            def keep_a(w):
                ac.wait_ge(M["sum_done"], w + 1)
                after(ac, M["turned"], w)
                ac.copy(mA[:, :], bank[0][:, :]).then_inc(M["mA"], 1)

            def copy_mT(w):
                ac.wait_ge(M["turned"], w + 1)
                after(ac, M["o_done"], w)
                ac.copy(mT[:, 0:4, :], bank[4][:, :].rearrange("p (c n) -> p c n", c=4)).then_inc(M["mT_a"], 1)

            peeled(ac, [(0, weigh), (1, copy_mT), (0, keep_a)])

        @block.vector
        def _(ve):
            ve.wait_ge(s_edge, 64)
            ve.tensor_scalar(hi_i[:, :], dst_i[:, :], 7, None, ALU.arith_shift_right)
            ve.tensor_scalar(lo_i[:, :], dst_i[:, :], 127, None, ALU.bitwise_and)
            ve.tensor_copy(dst_f[:, :], dst_i[:, :])
            for h in range(2):
                dg = dst_g[:, :].rearrange("p (q e) -> p q e", q=4)
                ve.tensor_reduce(ext[:, h, :], dg, X, ALU.min if h == 0 else ALU.max)
            ve.drain()
            ve.nop().then_inc(s_gext, 1)
            ve.tensor_copy(hi_f[:, :], hi_i[:, :])
            ve.tensor_copy(lo_f[:, :], lo_i[:, :])
            ve.wait_ge(s_cst, 6)
            ve.tensor_copy(iota[:, :], iota_i[:, :])
            ve.tensor_copy(pid[:, :], pid_i[:, :])
            ve.tensor_copy(asc[:, :], asc_i[:, :])
            ve.tensor_copy(wlo[:, :], wlo_i[:, :])
            ve.drain()
            ve.tensor_scalar(ident[:, :], iota[:, :], pid[:, 0:1], None, ALU.is_equal)
            ve.tensor_scalar(identh[:, :], iota[:, :], pid[:, 0:1], None, ALU.is_equal)
            ve.wait_ge(s_small, 16 * (len(bia) + 4 + 6 + 8))
            ve.tensor_tensor(bia["b0"][:, :], bia["b0"][:, :], bia["lb0"][:, :], ALU.add)
            ve.tensor_tensor(bia["b1"][:, :], bia["b1"][:, :], bia["lb1"][:, :], ALU.add)

            ve.wait_ge(s_extld, 16)
            ve.tensor_scalar(rcol[:, 4:5], wlo[:, :], float(P), None, ALU.add)
            ve.tensor_scalar(rtmp[:, :], asc[:, :], -1.0, float(NG + 1), ALU.mult, ALU.add)
            ve.drain()
            ve.scalar_tensor_tensor(out=rtmp2[:, :], in0=extb[:, 1, :], scalar=wlo[:, 0:1], in1=rtmp[:, :],
                                    op0=ALU.is_ge, op1=ALU.mult)
            ve.drain()
            ve.tensor_reduce(rcol[:, 5:6], rtmp2[:, :], X, ALU.max)
            ve.drain()
            ve.tensor_scalar(rcol[:, 6:7], rcol[:, 5:6], -1.0, float(NG), ALU.mult, ALU.add)
            ve.scalar_tensor_tensor(out=rtmp2[:, :], in0=extb[:, 0, :], scalar=rcol[:, 4:5], in1=asc[:, :],
                                    op0=ALU.is_lt, op1=ALU.mult)
            ve.drain()
            ve.tensor_scalar(rcol[:, 0:1], rcol[:, 6:7], float(NG - 2), None, ALU.min)
            ve.tensor_reduce(rcol[:, 5:6], rtmp2[:, :], X, ALU.max)
            ve.drain()
            ve.scalar_tensor_tensor(out=rcol[:, 1:2], in0=rcol[:, 0:1], scalar=2.0, in1=rcol[:, 5:6],
                                    op0=ALU.add, op1=ALU.max)
            ve.drain()
            ve.tensor_copy(rcol_i[:, :], rcol[:, 0:2]).then_inc(s_rcol, 1)

            for L in range(2):
                for i, k in enumerate((f"g{L}", f"be{L}")):
                    ve.tensor_reduce(bound[:, L, i:i + 1], bia[k][:, :], X, ALU.max, apply_absolute_value=True)
                ve.drain()
                ve.scalar_tensor_tensor(out=bound[:, L, 2:3], in0=bound[:, L, 0:1], scalar=22.7, in1=bound[:, L, 1:2],
                                        op0=ALU.mult, op1=ALU.add)
                ve.drain()
                ve.tensor_scalar(bound[:, L, 3:4], bound[:, L, 2:3], 1e-30, None, ALU.max)
                ve.drain()
                ve.tensor_scalar(bound[:, L, 4:5].bitcast(I32), bound[:, L, 3:4].bitcast(I32), 0x7F800000, None,
                                 ALU.bitwise_and)
                ve.drain()
                ve.tensor_scalar(bound[:, L, 5:6], bound[:, L, 4:5], 2.0 ** -14, None, ALU.mult)
                ve.drain()
                ve.reciprocal(bound[:, L, 6:7], bound[:, L, 5:6])
            ve.drain()

            def degree_onehots(j):
                for b in range(2):
                    if not isinstance(j, int):
                        ve.wait_ge(oh_used, j * 2 - 1 + b)
                    at = bass.ds((j * 2 + b) * 8, 8)
                    ve.tensor_tensor(ohl[:, b, :, :], iota[:, :].unsqueeze(1).broadcast_to([P, 8, P]),
                                     lo_f[:, at].unsqueeze(2).broadcast_to([P, 8, P]), ALU.is_equal)
                    ve.tensor_tensor(ohh[:, b, :, :], iota[:, 0:NW].unsqueeze(1).broadcast_to([P, 8, NW]),
                                     hi_f[:, at].unsqueeze(2).broadcast_to([P, 8, NW]), ALU.is_equal).then_inc(oh_rdy, 1)

            looped(ve, degree_onehots, NT // 16)
            ve.wait_ge(deg_sum, 1)
            ve.tensor_scalar(rdeg[:, :], bank[6][:, 0:NW], 1.0, None, ALU.add).then_inc(deg_ready, 1)
            ve.wait_ge(deg_sq, 1)
            ve.reciprocal(dinv[:, :], rdeg[:, :])
            ve.drain()
            for L in range(2):
                ve.tensor_scalar(dup[:, L, :], dinv[:, :], bound[:, L, 6:7], None, ALU.mult)
                ve.tensor_scalar(dse[:, L, :], dinv[:, :], bound[:, L, 5:6], None, ALU.mult)
                ve.tensor_scalar(rse[:, L, :], rdeg[:, :], bound[:, L, 5:6], None, ALU.mult)
            ve.drain()
            ve.nop().then_inc(deg_ready, 1)

            def stats(src, b):
                ve.bn_stats(st[:, b, :], src)
                ve.drain()
                return ve.bn_aggr(mv[:, b, 0:2], st[:, b, :])

            def scale(b, dcol=None):
                ve.reciprocal(mv[:, b, 3:4], mv[:, b, 2:3])
                ve.drain()
                if dcol is not None:
                    ve.tensor_tensor(mv[:, b, 3:4], mv[:, b, 3:4], dcol, ALU.mult)
                    ve.drain()
                return ve.scalar_tensor_tensor(out=mv[:, b, 4:5], in0=mv[:, b, 0:1], scalar=-1.0, in1=mv[:, b, 3:4],
                                               op0=ALU.mult, op1=ALU.mult)

            def affine(b, dst, g, be, dcol):
                ve.tensor_tensor(tn[:, b, :], tn[:, b, :], g[:, :], ALU.mult)
                ve.drain()
                return ve.scalar_tensor_tensor(out=dst, in0=be[:, :], scalar=dcol, in1=tn[:, b, :],
                                               op0=ALU.mult, op1=ALU.add)

            def norm_tiles(base, j, bs):
                for b in bs:
                    ve.wait_ge(x_in[b], (j + 1) * 16)
                    stats(xin[:, b, :], b).then_inc(n_st1, 1)
                for b in bs:
                    ve.wait_ge(n_sd1, base + 1 + b)
                    scale(b).then_inc(n_rs1, 1)
                for b in bs:
                    ve.wait_ge(n_h, base + 1 + b)
                    stats(hrel[:, b, :], b).then_inc(n_st2, 1)
                for b in bs:
                    ve.wait_ge(n_sd2, base + 1 + b)
                    scale(b, col(dup[:, 0, :], base + b)).then_inc(n_rs2, 1)
                for b in bs:
                    ve.wait_ge(n_g, base + 1 + b)
                    if not isinstance(j, int) or j > 0:
                        ve.wait_ge(n_out, base - 1 + b)
                    ve.scalar_tensor_tensor(out=t32[:, b, :], in0=bia["be0"][:, :], scalar=col(dup[:, 0, :], base + b),
                                            in1=tn[:, b, :], op0=ALU.mult, op1=ALU.add).then_inc(n_t32, 1)

            looped(ve, lambda j: norm_tiles(j * 2, j, (0, 1)), NW // 2)
            norm_tiles(NW - 1, NW // 2, (0,))
            ve.wait_ge(s_rld, 16)

            for L in range(2):
                S = G[L]
                c = ve.alloc_register(f"dve_gcn{L}_count")
                ve.reg_mov(c, 1)
                ve.tensor_copy(iota_w[:, :], iota[:, :])

                def onehots(w, S=S, c=c):
                    lo, hi = window_range(ve, w)
                    ve.drain()
                    with ve.Fori(lo, hi) as g:
                        n = ve.snap(c)
                        ve.wait_ge(S["used"], n)
                        ve.tensor_tensor(ohp[:, bass.ds(n % NB, 1), :, :].rearrange("p b k e -> p (b k) e"),
                                         iota_w[:, :].unsqueeze(1).broadcast_to([P, 2, P]),
                                         dst_f[:, bass.ds(g * 2, 2)].unsqueeze(2).broadcast_to([P, 2, P]),
                                         ALU.is_equal).then_inc(S["onehot"], 1)
                        ve.reg_add(c, c, 1)
                    ve.drain()
                    ve.tensor_scalar(iota_w[:, :], iota_w[:, :], float(P), None, ALU.add)

                def self_rows(w, S=S, L=L):
                    ve.wait_ge(S["self_high"], w + 1)
                    after(ve, S["turned"], w)
                    ve.scalar_tensor_tensor(out=hw[:, :], in0=tw[:, D:], scalar=col(rse[:, L, :], w), in1=hw0[:, :],
                                            op0=ALU.mult, op1=ALU.add).then_inc(S["self_done"], 1)

                def copy_at(w, S=S):
                    ve.wait_ge(S["turned"], w + 1)
                    after(ve, S["dense_done"], w)
                    ve.tensor_copy(AT[:, 4:8, :], bank[2][:, :].rearrange("p (c n) -> p c n", c=4)).then_inc(S["at_b"], 1)

                def add_bias(w, S=S, L=L):
                    ve.wait_ge(S["dense_done"], w + 1)
                    after(ve, S["relu_done"], w)
                    ve.tensor_tensor(yb[:, :], bank[3][:, :], bia["b0" if L == 0 else "b1"][:, :],
                                     ALU.add).then_inc(S["y_read"], 1)

                def second_norm(w, S=S):
                    ve.wait_ge(S["relu_done"], w + 1)
                    stats(r[:, :], 0).then_inc(S["stats"], 1)
                    ve.wait_ge(S["std"], w + 1)
                    scale(0, col(dup[:, 1, :], w)).then_inc(S["scale"], 1)
                    ve.wait_ge(S["tn"], w + 1)
                    affine(0, t32[:, 0, :], bia["g1"], bia["be1"], col(dup[:, 1, :], w)).then_inc(S["t32"], 1)
                    ve.wait_ge(S["high"], w + 1)
                    ve.tensor_tensor(tout[:, 0, D:], t32[:, 0, :], tout[:, 0, 0:D], ALU.subtract).then_inc(S["tout"], 1)

                def project_in(w, S=S):
                    ve.wait_ge(S["relu_done"], w + 1)
                    ve.wait_ge(S["r0_in"], (w + 1) * 16)
                    after(ve, S["xs_turned"], w)
                    ve.tensor_tensor(xs[:, :], r[:, :], r0w[:, :], ALU.add).then_inc(S["xs_ready"], 1)

                def residual(w, S=S):
                    ve.wait_ge(S["x_in"], (w + 1) * 16)
                    ve.wait_ge(S["proj_done"], w + 1)
                    after(ve, S["x1_stored"], w, 16)
                    after(ve, S["h_ready"], w)
                    ve.tensor_tensor(x1[:, :], bank[5][:, :], bia["pb"][:, :], ALU.add)
                    ve.drain()
                    ve.tensor_tensor(x1[:, :], x1[:, :], xw[:, :], ALU.add).then_inc(S["x1_ready"], 1)
                    ve.drain()
                    stats(x1[:, :], 0).then_inc(S["stats"], 1)
                    ve.wait_ge(S["std"], w + 1)
                    scale(0).then_inc(S["scale"], 1)

                if L == 0:
                    peeled(ve, [(0, onehots), (2, add_bias), (1, copy_at), (0, self_rows), (2, second_norm)])
                else:
                    peeled(ve, [(0, onehots), (2, add_bias), (1, copy_at), (0, self_rows), (2, project_in), (2, residual)])

            c = ve.alloc_register("dve_tp_count")
            ve.reg_mov(c, 1)
            ve.wait_ge(G[1]["x1_stored"], 16 * NW)
            ve.wait_ge(G[1]["up_ready"], NW)
            ve.nop().then_inc(M["msg_ready"], 2)
            ve.nop().then_inc(M["u_used"], 2)
            ve.tensor_copy(iota_w[:, :], iota[:, :])

            def messages(w):
                lo, hi = window_range(ve, w)
                ve.drain()
                with ve.Fori(lo, hi) as g:
                    n = ve.snap(c)

                    def pair(b):
                        u = ring_u[:, b, :, :]
                        ve.wait_ge(M["q0"], n)
                        for k in range(2):
                            ve.scalar_tensor_tensor(out=q1[:, k, :], in0=u[:, k, 2 * P:3 * P],
                                                    scalar=yg[:, b, 4 * k + 2:4 * k + 3],
                                                    in1=q0[:, b, k, :], op0=ALU.mult, op1=ALU.add)
                        ve.wait_ge(M["w_done"], n + 2)
                        if True:
                            for k in range(2):
                                ve.tensor_tensor(t2[:, k, :], w_bank[k][1][:, 0:P], u[:, k, 0:P], ALU.mult)
                        ve.drain()
                        ve.nop().then_inc(M["t2"], 1)
                        for k in range(2):
                            ve.scalar_tensor_tensor(out=q2[:, k, :], in0=u[:, k, 3 * P:4 * P],
                                                    scalar=yg[:, b, 4 * k + 3:4 * k + 4],
                                                    in1=q1[:, k, :], op0=ALU.mult, op1=ALU.add)
                        ve.wait_ge(M["seg_done"], n)
                        ve.tensor_tensor(oh[:, b, :, :], iota_w[:, :].unsqueeze(1).broadcast_to([P, 2, P]),
                                         dst_f[:, bass.ds(g * 2, 2)].unsqueeze(2).broadcast_to([P, 2, P]), ALU.is_equal)
                        ve.wait_ge(M["w13"], n)
                        for k in range(2):
                            ve.tensor_tensor(msg[:, b, k, 0, 0:P], w13[:, k, 0:P], u[:, k, 0:P], ALU.mult)
                            ve.tensor_tensor(msg[:, b, k, 0, P:].rearrange("p (m u) -> p m u", m=3),
                                             w13[:, k, P:2 * P].unsqueeze(1).broadcast_to([P, 3, P]),
                                             u[:, k, P:4 * P].rearrange("p (m u) -> p m u", m=3), ALU.mult)
                        ve.drain()
                        ve.nop().then_inc(M["u_used"], 1)
                        for k in range(2):
                            ve.tensor_tensor(msg[:, b, k, 1, 0:P], q2[:, k, :], w_bank[k][1][:, P:2 * P], ALU.mult)
                        ve.drain()
                        ve.wait_ge(M["p2"], n)
                        ve.nop().then_inc(M["msg_ready"], 1)
                        ve.reg_add(c, c, 1)
                    pick(ve, ve.snap(n % 2), 0, 2, pair)
                ve.drain()
                ve.tensor_scalar(iota_w[:, :], iota_w[:, :], float(P), None, ALU.add)

            def keep_b(w):
                ve.wait_ge(M["sum_done"], w + 1)
                after(ve, M["turned"], w)
                ve.tensor_copy(mB[:, :], bank[1][:, :]).then_inc(M["mB"], 1)

            def copy_mT(w):
                ve.wait_ge(M["turned"], w + 1)
                after(ve, M["o_done"], w)
                ve.tensor_copy(mT[:, 4:8, :], m_bank[1][:, :].rearrange("p (c n) -> p c n", c=4)).then_inc(M["mT_b"], 1)

            def finish(w):
                ve.wait_ge(M["x1_in"], (w + 1) * 16)
                ve.wait_ge(M["o_done"], w + 1)
                after(ve, M["stored"], w, 16)
                ve.tensor_tensor(x1[:, 0:P], xw[:, 0:P], bank[6][:, 0:P], ALU.add)
                ve.tensor_tensor(x1[:, P:].rearrange("p (v m) -> p v m", m=3), xw[:, P:].rearrange("p (v m) -> p v m", m=3),
                                 bank[6][:, P:].rearrange("p (m v) -> p v m", m=3), ALU.add).then_inc(M["out_ready"], 1)

            peeled(ve, [(0, messages), (1, copy_mT), (0, keep_b), (1, finish)])

        @block.tensor
        def _(pe):
            pe.wait_ge(s_wsc, 1)

            def touch(t, n, start):
                return pe.matmul(t, zeros[:, 0:P], zeros[:, 0:n], start=start, stop=not start, skip_group_check=True)

            def degrees(j, b):
                pe.wait_ge(oh_rdy, j * 2 + 1 + b)
                for t in range(8):
                    ins = pe.matmul(bank[6][:, 0:NW], ohl[:, b, t, :], ohh[:, b, t, :], start=False, stop=False,
                                    skip_group_check=True)
                ins.then_inc(oh_used, 1)

            def radial(j):
                for b in range(2):
                    pe.wait_ge(ef_in[b], j * 16 + 16)
                    pe.matmul(bank[0 + b][:, :], w1[:, :], ef[:, b, :], start=True, stop=True).then_inc(m1, 1)
                degrees(j, 0)
                for b in range(2):
                    pe.wait_ge(a1, j * 2 + 1 + b)
                    pe.matmul(bank[2 + b][:, :], w2[:, :], hA[:, b, :], start=True, stop=True).then_inc(m2, 1)
                degrees(j, 1)
                for b in range(2):
                    pe.wait_ge(a2, j * 2 + 1 + b)
                    if not isinstance(j, int):
                        pe.wait_ge(a3, j * 2 - 1 + b)
                    pe.matmul(bank[4 + b][:, :], w3[:, :], hB[:, b, :], start=True, stop=True).then_inc(m3, 1)

            touch(bank[6][:, 0:NW], NW, True)
            looped(pe, radial, NG // 8)
            touch(bank[6][:, 0:NW], NW, False).then_inc(deg_sum, 1)
            pe.wait_ge(s_big, 16 * len(W))
            pe.wait_ge(a3, NG // 4)
            pe.wait_ge(deg_ready, 1)
            pe.wait_ge(s_rld, 16)

            for L in range(2):
                S = G[L]
                WC, WL = (W["W0"], W["lw0"]) if L == 0 else (W["W1"], W["lw1"])
                c = pe.alloc_register(f"pe_gcn{L}_count")
                pe.reg_mov(c, 1)
                pe.nop().then_inc(S["used"], NB)

                def edge_sum(w, S=S, c=c):
                    lo, hi = window_range(pe, w)
                    after(pe, S["agg_ready"], w)
                    touch(bank[0][:, :], D, True)
                    with pe.Fori(lo, hi) as g:
                        n = pe.snap(c)
                        pe.wait_ge(S["onehot"], n)

                        def add(b):
                            pe.wait_ge(S["got"][b], pe.snap((n + (NB - 1)) // NB * 32))
                            for k in range(2):
                                for h in range(2):
                                    ins = pe.matmul(bank[0][:, :], ohp[:, b, k, :], ring_h[:, b, k, h * D:(h + 1) * D],
                                                    start=False, stop=False, skip_group_check=True)
                            ins.then_inc(S["used"], 1)
                        pick(pe, pe.snap(n % NB), 0, NB, add)
                        pe.reg_add(c, c, 1)
                    pe.wait_ge(S["self_in"], (w + 1) * 16)
                    for h in range(2):
                        ins = pe.matmul(bank[0][:, :], identh[:, :], tw[:, h * D:(h + 1) * D], start=False, stop=(h == 1),
                                        skip_group_check=True)
                    ins.then_inc(S["sum_done"], 1)

                def turn(w, S=S):
                    pe.wait_ge(S["agg_ready"], w + 1)
                    pe.wait_ge(S["self_done"], w + 1)
                    after(pe, S["at_a"], w)
                    after(pe, S["at_b"], w)
                    for i in range(8):
                        sr = (agg if i < 4 else hw)[:, (i % 4) * P:(i % 4 + 1) * P]
                        ins = pe.transpose(bank[1 + i // 4][:, (i % 4) * P:(i % 4 + 1) * P], sr, ident[:, :])
                    ins.then_inc(S["turned"], 1)

                def dense(w, S=S, WC=WC, WL=WL):
                    pe.wait_ge(S["at_a"], w + 1)
                    pe.wait_ge(S["at_b"], w + 1)
                    after(pe, S["y_read"], w)
                    for i in range(8):
                        ins = pe.matmul(bank[3][:, :], AT[:, i, :], (WC if i < 4 else WL)[:, i % 4, :],
                                        start=(i == 0), stop=(i == 7))
                    ins.then_inc(S["dense_done"], 1)

                def turn_xs(w, S=S):
                    pe.wait_ge(S["xs_ready"], w + 1)
                    after(pe, S["xT_ready"], w)
                    for i in range(4):
                        ins = pe.transpose(bank[4][:, i * P:(i + 1) * P], xs[:, i * P:(i + 1) * P], ident[:, :])
                    ins.then_inc(S["xs_turned"], 1)

                def project(w, S=S):
                    pe.wait_ge(S["xT_ready"], w + 1)
                    after(pe, S["x1_ready"], w)
                    for i in range(4):
                        ins = pe.matmul(bank[5][:, :], xT[:, i, :], W["pw"][:, i, :], start=(i == 0), stop=(i == 3))
                    ins.then_inc(S["proj_done"], 1)

                def turn_h(w, S=S):
                    pe.wait_ge(S["h_ready"], w + 1)
                    after(pe, S["hT_ready"], w)
                    for i in range(4):
                        sr = hrel[:, 0, 0:P] if i == 0 else hrel[:, 0, P:].rearrange("p (u m) -> p m u", m=3)[:, i - 1, :]
                        ins = pe.transpose(bank[6][:, i * P:(i + 1) * P], sr, ident[:, :])
                    ins.then_inc(S["h_turned"], 1)

                def up(w, S=S):
                    pe.wait_ge(S["hT_ready"], w + 1)
                    after(pe, S["up_ready"], w)
                    for i in range(4):
                        ins = pe.matmul(bank[7][:, i * P:(i + 1) * P], hT[:, i, :], wup[:, min(i, 1), :], start=True, stop=True)
                    ins.then_inc(S["up_done"], 1)

                if L == 0:
                    peeled(pe, [(0, edge_sum), (1, turn), (1, dense), (2, lambda w: None)])
                else:
                    peeled(pe, [(0, edge_sum), (3, turn_h), (1, turn), (3, up), (1, dense), (2, turn_xs), (2, project)])

            c = pe.alloc_register("pe_tp_count")
            pe.reg_mov(c, 1)
            pe.wait_ge(G[1]["up_ready"], NW)
            pe.wait_ge(G[1]["agg_ready"], NW)
            pe.wait_ge(G[1]["x1_ready"], NW)
            pe.nop().then_inc(M["w_done"], 2)
            pe.nop().then_inc(M["seg_done"], 2)

            def edge_weights(n, b):
                pe.wait_ge(M["hid_in"][b], pe.snap((n + 1) // 2 * 16))
                pe.wait_ge(M["msg_ready"], n + 1)
                for h in range(2):
                    for k in range(2):
                        ins = pe.matmul(w_bank[k][h][:, 0:2 * P], hid[k * HID:(k + 1) * HID, b, :],
                                        w4[k * HID:(k + 1) * HID, h * 2 * P:(h + 1) * 2 * P], start=True, stop=True)
                ins.then_inc(M["w_done"], 1)

            def sum_pair(n, b):
                pe.wait_ge(M["msg_ready"], n + 2)
                for k in range(2):
                    for h in range(2):
                        ins = pe.matmul(bank[h][:, :], oh[:, b, k, :], msg[:, b, k, h, :], start=False, stop=False,
                                        skip_group_check=True)
                ins.then_inc(M["seg_done"], 1)

            def pair_sums(w):
                lo, hi = window_range(pe, w)
                after(pe, M["mA"], w)
                after(pe, M["mB"], w)
                touch(bank[0][:, :], D, True)
                touch(bank[1][:, :], D, True)
                n = pe.snap(c)
                pick(pe, pe.snap(n % 2), 0, 2, lambda b: edge_weights(n, b))
                pe.reg_add(c, c, 1)
                with pe.Fori(lo + 1, hi) as g:
                    n = pe.snap(c)

                    def step(b):
                        edge_weights(n, b)
                        sum_pair(n - 1, 1 - b)
                    pick(pe, pe.snap(n % 2), 0, 2, step)
                    pe.reg_add(c, c, 1)
                n = pe.snap(c)
                pick(pe, pe.snap(n % 2), 0, 2, lambda b: sum_pair(n - 1, 1 - b))
                touch(bank[0][:, :], D, False)
                touch(bank[1][:, :], D, False).then_inc(M["sum_done"], 1)

            def turn_m(w):
                pe.wait_ge(M["mA"], w + 1)
                pe.wait_ge(M["mB"], w + 1)
                after(pe, M["mT_a"], w)
                after(pe, M["mT_b"], w)
                after(pe, M["out_ready"], w)
                for i in range(8):
                    sr = (mA if i < 4 else mB)[:, (i % 4) * P:(i % 4 + 1) * P]
                    ins = pe.transpose(m_bank[i // 4][:, (i % 4) * P:(i % 4 + 1) * P], sr, ident[:, :])
                ins.then_inc(M["turned"], 1)

            def out_product(w):
                pe.wait_ge(M["mT_a"], w + 1)
                pe.wait_ge(M["mT_b"], w + 1)
                after(pe, M["out_ready"], w)
                for i in range(4):
                    first, second = (0, 4) if i == 0 else (4 + i, i)
                    o = bank[6][:, i * P:(i + 1) * P]
                    pe.matmul(o, mT[:, first, :], wo[:, 0 if i == 0 else 2, :], start=True, stop=False)
                    ins = pe.matmul(o, mT[:, second, :], wo[:, 1 if i == 0 else 3, :], start=False, stop=True)
                ins.then_inc(M["o_done"], 1)

            peeled(pe, [(0, pair_sums), (1, turn_m), (1, out_product)])


_SHORT = {"W0": "L0_gnn_W0", "b0": "L0_gnn_b0", "lb0": "L0_gnn_lb0", "g0": "L0_gnn_g0", "be0": "L0_gnn_be0",
          "W1": "L0_gnn_W1", "b1": "L0_gnn_b1", "lb1": "L0_gnn_lb1", "g1": "L0_gnn_g1", "be1": "L0_gnn_be1",
          "pb": "L0_gnn_pb", "W_up0": "L1_gnn_W_up0", "W_up1": "L1_gnn_W_up1", "W_mlp1": "L1_gnn_W_mlp1",
          "W_mlp2": "L1_gnn_W_mlp2", "W_mlp3": "L1_gnn_W_mlp3", "W_mlp4": "L1_gnn_W_mlp4",
          "W_out0": "L1_gnn_W_out0", "W_out1": "L1_gnn_W_out1", "x": "x"}


def kernel(**inputs):
    import numpy as _np
    import concourse.bacc as _bacc
    from concourse import mybir as _mybir
    from concourse.bass_utils import run_bass_kernel_spmd as _run

    nc = _bacc.Bacc("TRN2", target_bir_lowering=False, num_devices=1)
    laid = {k: _np.asarray(inputs[v]) for k, v in _SHORT.items()}
    for k, v in (("lw0", "L0_gnn_lw0"), ("lw1", "L0_gnn_lw1"), ("pw", "L0_gnn_pw")):
        laid[k] = _np.asarray(inputs[v]).T
    pad = NT * P - E
    src, dst = _np.asarray(inputs["src"]), _np.asarray(inputs["dst"])
    ea, ef = _np.asarray(inputs["edge_attr_4"]), _np.asarray(inputs["edge_attr_8"])
    laid["src_t"] = _np.pad(src, (0, pad)).reshape(NT, P).T
    laid["dst_t"] = _np.pad(dst, (0, pad), constant_values=-1).reshape(NT, P).T
    laid["dst_g"] = _np.pad(dst, (0, pad), mode="edge").reshape(NG // 4, 4 * 256)
    laid["ea_t"] = _np.pad(ea, ((0, pad), (0, 0))).reshape(NT, P, 4).transpose(1, 0, 2).reshape(P, NT * 4)
    laid["ef_t"] = (_np.pad(ef, ((0, pad), (0, 0))).reshape(NG, 2, P, RB).transpose(1, 3, 0, 2)
                    .reshape(2 * RB, NG * P))
    arrays, args = {}, {}
    for name, v in laid.items():
        v = _np.ascontiguousarray(v)
        arrays[f"in_{name}_dram"] = v
        args[name] = nc.dram_tensor(f"in_{name}_dram", v.shape, _mybir.dt.from_np(v.dtype), kind="ExternalInput").ap()
    out = nc.dram_tensor("out_0_dram", (N, D), _mybir.dt.float32, kind="ExternalOutput").ap()
    build(nc, args, out)
    r = _run(nc, [arrays], core_ids=[0])
    return r.results[0]["out_0_dram"]
```

```python
from contextlib import ExitStack

import concourse.bass as bass
from concourse import mybir

P = 128
N, D, E = 6250, 512, 100000
NW = (N + P - 1) // P
NPAD = NW * P
TAIL = N - (NW - 1) * P
NT = 784
NG = NT // 2
NB = 8
NF = 4
NU = 4
KC = D // P
HID = 64
RB = 8
EPS = 1e-5
SILU_2MOM = 1.679177
AVG = 10.0

ALU = mybir.AluOpType
ACT = mybir.ActivationFunctionType
F32 = mybir.dt.float32
BF16 = mybir.dt.bfloat16
F16 = mybir.dt.float16
I32 = mybir.dt.int32
X = mybir.AxisListType.X


def build(nc, a, out):
    with ExitStack() as ctx:
        def sb(name, shape, dt=F32):
            return ctx.enter_context(nc.sbuf_tensor(name, shape, dt))

        def sem(name):
            return ctx.enter_context(nc.semaphore(name))

        def dram(name, shape, dt=F32):
            return nc.dram_tensor(name, shape, dt).ap()

        hid_d = dram("hid_d", (NG, P, P))
        tab_d = [dram("tab0_d", (NPAD, 2 * D), F16), dram("tab1_d", (NPAD, 2 * D), F16)]
        r0_d = dram("r0_d", (NPAD, D))
        x1_d = dram("x1_d", (NPAD, D))
        up_d = dram("up_d", (NPAD, D))
        ext_d = dram("ext_d", (2, NG))
        rng_d = dram("rng_d", (NW, 2), I32)

        bank = [ctx.enter_context(nc.psum_tensor(f"bank{i}", [P, D], F32)) for i in range(8)]

        src_i = sb("src_i", [P, NT], I32)
        dst_f = sb("dst_f", [P, NT])
        y_t = sb("y_t", [P, NT * 4])
        ident = sb("ident", [P, P])
        iota = sb("iota", [P, P])
        iota_w = sb("iota_w", [P, P])
        zeros = sb("zeros", [P, D], BF16)
        eps = sb("eps", [P, 1])
        rdeg = sb("rdeg", [P, NW])
        dinv = sb("dinv", [P, NW])
        dinv2 = sb("dinv2", [P, NW])
        rng = sb("rng", [1, 2 * NW], I32)
        dup = sb("dup", [P, 2, NW])
        dse = sb("dse", [P, 2, NW])
        rse = sb("rse", [P, 2, NW])
        bound = sb("bound", [P, 2, 8])
        dense_w = sb("dense_w", [P, 5, KC, D])
        W = {k: dense_w[:, i, :, :] for i, k in enumerate(("W0", "lw0", "W1", "lw1", "pw"))}
        wup = sb("wup", [P, 2, P])
        w1 = sb("w1", [2 * RB, P])
        w2 = sb("w2", [P, P])
        w3 = sb("w3", [P, P])
        w4 = sb("w4", [P, D])
        wo = sb("wo", [P, 4, P])
        bia = {k: sb("v_" + k, [P, D]) for k in ("b0", "lb0", "g0", "be0", "b1", "lb1", "g1", "be1", "pb")}

        ring = sb("ring", [P, NB * 2 * D])
        ring_h = ring[:, :].bitcast(F16).rearrange("p (b k n) -> p b k n", b=NB, k=2)
        ring_u = ring[:, 0:NU * 2 * D].rearrange("p (b k n) -> p b k n", b=NU, k=2)
        early = [ring[:, i * NT:(i + 1) * NT] for i in range(5)]
        dst_i, hi_i, lo_i = (t.bitcast(I32) for t in early[0:3])
        hi_f, lo_f = early[3:5]
        dst_g = ring[0:NG // 4, 5 * NT:5 * NT + 1024].bitcast(I32)
        ohl = sb("ohl", [P, 2, 8, P], BF16)
        ohh = sb("ohh", [P, 2, 8, NW], BF16)
        ext = sb("ext", [NG // 4, 2, 4])
        extb = sb("extb", [NW, 2, NG])
        asc = sb("asc", [NW, NG])
        asc_i = sb("asc_i", [NW, NG], I32)
        rtmp = sb("rtmp", [NW, NG])
        rtmp2 = sb("rtmp2", [NW, NG])
        wlo = sb("wlo", [NW, 1])
        wlo_i = sb("wlo_i", [NW, 1], I32)
        rcol = sb("rcol", [NW, 8])
        rcol_i = sb("rcol_i", [NW, 2], I32)
        iota_i = sb("iota_i", [P, P], I32)
        pid_i = sb("pid_i", [P, 1], I32)
        pid = sb("pid", [P, 1])
        ef = sb("ef", [2 * RB, 2, D])
        hA = sb("hA", [P, 2, D])
        hB = sb("hB", [P, 2, D])
        hC = sb("hC", [P, 2, D])

        xin = sb("xin", [P, 2, D])
        hrel = sb("hrel", [P, 2, D])
        tn = sb("tn", [P, 2, D])
        t32 = sb("t32", [P, 2, D])
        tout = sb("tout", [P, 2, 2 * D], F16)
        st = sb("st", [P, 2, 6])
        mv = sb("mv", [P, 2, 8])

        ohp = sb("ohp", [P, NB, 2, P], F16)
        oh = sb("oh", [P, 2, 2, P])
        ohp_k = ohp[:, :, :, :].rearrange("p b k n -> p (b k) n")
        ring_k = ring[:, :].bitcast(F16).rearrange("p (b n) -> p b n", n=D)
        idx = sb("idx", [P, NB, 2], I32)
        tw = sb("tw", [P, 2 * D], F16)
        hw0 = xin[:, 0, :]
        hw = sb("hw", [P, D])
        agg = sb("agg", [P, D])
        AT = sb("AT", [P, 8, P])
        yb = sb("yb", [P, D])
        r = sb("r", [P, D])
        r0w = sb("r0w", [P, D])
        xs = sb("xs", [P, D])
        xT = sb("xT", [P, KC, P])
        xw = sb("xw", [P, D])
        x1 = sb("x1", [P, D])
        hT = sb("hT", [P, KC, P])
        uo = sb("uo", [P, D])

        msg = dense_w[:, 0:2, :, :].rearrange("p a (k h) n -> p a k h n", k=2)
        hid = hC[:, 0, 0:256].rearrange("p (b n) -> p b n", b=2)
        yg = hC[:, 1, 0:16].rearrange("p (b n) -> p b n", b=2)
        w13 = hA[:, 0, :].rearrange("p (k n) -> p k n", k=2)
        t2, q1 = (hA[:, 1, i * 256:(i + 1) * 256].rearrange("p (k n) -> p k n", k=2) for i in range(2))
        q2 = hB[:, 0, 0:256].rearrange("p (k n) -> p k n", k=2)
        q0 = hB[:, 1, :].rearrange("p (b k n) -> p b k n", b=2, k=2)
        mA, mB, mT = agg, hw, AT

        def s(name):
            return sem(name)

        s_edge, s_small, s_big = s("edges_in"), s("small_weights_in"), s("big_weights_in")
        s_gext, s_extst, s_extld, s_rst, s_rld = (s("ext_ready"), s("ext_stored"), s("ext_loaded"),
                                                  s("ranges_stored"), s("ranges_loaded"))
        s_cst, s_wz, s_wsc, s_rcol = s("constants_ready"), s("weights_zeroed"), s("weights_scaled"), s("ranges_ready")
        ef_in = [s(f"ef_in{i}") for i in range(2)]
        hid_out = [s(f"hid_out{i}") for i in range(2)]
        m1, m2, m3 = s("radial1_sum"), s("radial2_sum"), s("radial3_sum")
        a1, a2, a3 = s("radial1_act"), s("radial2_act"), s("radial3_act")
        oh_rdy, oh_used = s("degree_onehot_ready"), s("degree_onehot_used")
        deg_sum, deg_ready, deg_sq = s("degree_summed"), s("dinv_ready"), s("degree_root")
        x_in = [s(f"x_in{i}") for i in range(2)]
        t_st = [s(f"table0_stored{i}") for i in range(2)]
        n_st1, n_sd1, n_rs1, n_h, n_st2, n_sd2, n_rs2, n_t, n_out = (
            s("norm_stats1"), s("norm_std1"), s("norm_scale1"), s("norm_relu"), s("norm_stats2"),
            s("norm_std2"), s("norm_scale2"), s("norm_table_scaled"), s("norm_table_ready"))
        n_g, n_t32, n_hi = s("norm_times_g"), s("norm_table_f32"), s("norm_table_high")

        def peeled(eng, stages):
            depth = max(d for d, _ in stages)
            for w in range(depth + 1):
                for d, f in stages:
                    if w - d >= 0:
                        f(w - d)
            with eng.Fori(depth + 1, NW) as w:
                for d, f in stages:
                    f(w - d)
            for w in range(NW, NW + depth):
                for d, f in stages:
                    if w - d < NW:
                        f(w - d)

        def after(eng, sm, w, per=1):
            if isinstance(w, int):
                if w > 0:
                    eng.wait_ge(sm, w * per)
            else:
                eng.wait_ge(sm, w * per)

        def looped(eng, body, n):
            body(0)
            with eng.Fori(1, n) as i:
                body(i)

        def rows(t, w):
            return t[w * P:(w + 1) * P, :] if isinstance(w, int) else t[bass.ds(w * P, P), :]

        def col(t, w):
            return t[:, w:w + 1] if isinstance(w, int) else t[:, bass.ds(w, 1)]

        def window_range(eng, w):
            at = w * 2
            if isinstance(w, int):
                la, ha = rng[0:1, at:at + 1], rng[0:1, at + 1:at + 2]
            else:
                la, ha = rng[0:1, bass.ds(at, 1)], rng[0:1, bass.ds(w * 2 + 1, 1)]
            return eng.value_load(la, min_val=0, max_val=NG - 2), eng.value_load(ha, min_val=2, max_val=NG)

        def pick(eng, sel, lo, hi, body):
            if hi - lo == 1:
                body(lo)
                return
            mid = (lo + hi) // 2
            with eng.If(sel < mid):
                pick(eng, sel, lo, mid, body)
            with eng.Else():
                pick(eng, sel, mid, hi, body)

        def over_windows(eng, window):
            window(0)
            window(1)
            with eng.Fori(2, NW - 1) as w:
                window(w)
            window(NW - 1)

        block = ctx.enter_context(nc.Block())

        def gcn_sems(L):
            names = ("used", "onehot", "arrived", "sum_done", "agg_ready", "self_in", "self_high", "self_done",
                     "turned", "at_a", "at_b", "dense_done", "y_read", "relu_done", "r_stored", "tab_stored",
                     "stats", "std", "scale", "tn", "t32", "high", "tout", "r0_in", "xs_ready", "xs_turned", "xT_ready",
                     "proj_done", "x_in", "x1_ready", "x1_stored", "h_ready", "h_turned", "hT_ready", "up_done",
                     "up_ready", "up_stored")
            S = {k: s(f"gcn{L}_{k}") for k in names}
            S["got"] = [s(f"gcn{L}_gathered{k}") for k in range(NF)]
            return S

        G = [gcn_sems(0), gcn_sems(1)]
        w_bank = [[bank[2], bank[3]], [bank[7], bank[5]]]
        m_bank = [bank[4], bank[6]]
        M = {k: s("tp_" + k) for k in (
            "idx_ready", "w_done", "w13", "t2", "q0", "p2", "u_used", "w_read", "onehot", "seg_done",
            "sum_done", "mA", "mB", "turned", "mT_a", "mT_b", "o_done", "x1_in", "out_ready", "stored")}
        M["got"] = [s(f"tp_gathered{k}") for k in range(NU)]
        M["hid_in"] = [s(f"tp_hidden_in{k}") for k in range(2)]

        @block.sync
        def _(sp):
            for t, k in ((src_i[:, :], "src_t"), (dst_i, "dst_t"), (dst_g, "dst_g"), (y_t[:, :], "ea_t")):
                sp.dma_start(t, a[k]).then_inc(s_edge, 16)
            for k in bia:
                sp.dma_start(bia[k][:, :], a[k].rearrange("(a d) -> a d", a=1).broadcast_to([P, D])).then_inc(s_small, 16)
            sp.dma_start(wup[:, 0, :], a["W_up0"]).then_inc(s_small, 16)
            sp.dma_start(wup[:, 1, :], a["W_up1"]).then_inc(s_small, 16)
            sp.dma_start(wo[:, 0:2, :], a["W_out0"].rearrange("(c p) n -> p c n", p=P)).then_inc(s_small, 16)
            sp.dma_start(wo[:, 2:4, :], a["W_out1"].rearrange("(c p) n -> p c n", p=P)).then_inc(s_small, 16)
            sp.wait_ge(s_wz, 3)
            for t, k, n in ((w1, "W_mlp1", RB), (w2, "W_mlp2", HID), (w3, "W_mlp3", HID)):
                for h in range(2):
                    sp.dma_start(t[h * n:(h + 1) * n, h * HID:(h + 1) * HID], a[k]).then_inc(s_small, 16)
            for h in range(2):
                for c, f in enumerate((0, 2, 1, 3)):
                    sp.dma_start(w4[h * HID:(h + 1) * HID, c * P:(c + 1) * P],
                                 a["W_mlp4"][:, f * P:(f + 1) * P]).then_inc(s_small, 16)
            sp.wait_ge(s_gext, 1)
            sp.dma_start(ext_d.rearrange("a (p q) -> p a q", q=4), ext[:, :, :]).then_inc(s_extst, 16)
            for k in W:
                sp.dma_start(W[k][:, :, :], a[k].rearrange("(c p) n -> p c n", p=P)).then_inc(s_big, 16)
            sp.wait_ge(s_extst, 16)
            sp.dma_start(extb[:, :, :], ext_d.rearrange("(o a) g -> o a g", o=1).broadcast_to([NW, 2, NG])).then_inc(s_extld, 16)
            sp.wait_ge(s_rcol, 1)
            sp.dma_start(rng_d, rcol_i[:, :]).then_inc(s_rst, 16)
            sp.wait_ge(s_rst, 16)
            sp.dma_start(rng[:, :], rng_d.rearrange("(o w) k -> o (w k)", o=1)).then_inc(s_rld, 16)

            def load_x(j):
                for b in range(2):
                    if not isinstance(j, int) or j > 0:
                        sp.wait_ge(n_h, j * 2 - 1 + b)
                    sp.dma_start(xin[:, b, :], a["x"][bass.ds((j * 2 + b) * P, P), :]).then_inc(x_in[b], 16)

            def store_table(j):
                for b in range(2):
                    sp.wait_ge(n_out, j * 2 + 1 + b)
                    sp.dma_start(tab_d[0][bass.ds((j * 2 + b) * P, P), :], tout[:, b, :]).then_inc(t_st[b], 16)

            load_x(0)
            with sp.Fori(0, NW // 2 - 1) as j:
                load_x(j + 1)
                store_table(j)
            sp.wait_ge(n_h, NW - 2)
            sp.dma_start(xin[0:TAIL, 0, :], a["x"][N - TAIL:N, :]).then_inc(x_in[0], 16)
            store_table(NW // 2 - 1)
            sp.wait_ge(n_out, NW)
            sp.dma_start(tab_d[0][(NW - 1) * P:, :], tout[:, 0, :]).then_inc(t_st[0], 16)
            sp.wait_ge(t_st[0], 16 * (NW // 2 + 1))
            sp.wait_ge(t_st[1], 16 * (NW // 2))

            for L in range(2):
                S = G[L]

                def self_rows(w, S=S, L=L):
                    after(sp, S["self_done"], w)
                    sp.dma_start(tw[:, :], rows(tab_d[L], w)).then_inc(S["self_in"], 16)

                def store_r(w, S=S):
                    sp.wait_ge(S["relu_done"], w + 1)
                    sp.dma_start(rows(r0_d, w), r[:, :]).then_inc(S["r_stored"], 16)

                def store_tab(w, S=S):
                    sp.wait_ge(S["tout"], w + 1)
                    sp.dma_start(rows(tab_d[1], w), tout[:, 0, :]).then_inc(S["tab_stored"], 16)

                def load_r0(w, S=S):
                    after(sp, S["xs_ready"], w)
                    sp.dma_start(r0w[:, :], rows(r0_d, w)).then_inc(S["r0_in"], 16)

                def load_x(w, S=S):
                    after(sp, S["x1_ready"], w)
                    if isinstance(w, int) and w == NW - 1:
                        sp.dma_start(xw[0:TAIL, :], a["x"][N - TAIL:N, :]).then_inc(S["x_in"], 16)
                    else:
                        sp.dma_start(xw[:, :], rows(a["x"], w)).then_inc(S["x_in"], 16)

                def store_x1(w, S=S):
                    sp.wait_ge(S["x1_ready"], w + 1)
                    sp.dma_start(rows(x1_d, w), x1[:, :]).then_inc(S["x1_stored"], 16)

                def store_up(w, S=S):
                    sp.wait_ge(S["up_ready"], w + 1)
                    sp.dma_start(rows(up_d, w), uo[:, :]).then_inc(S["up_stored"], 16)

                c = sp.alloc_register(f"sp_gcn{L}_count")
                sp.reg_mov(c, 1)

                def relay(w, S=S, c=c):
                    lo, hi = window_range(sp, w)
                    with sp.Fori(lo, hi) as g:
                        n = sp.snap(c)

                        def arrived(b):
                            sp.wait_ge(S["got"][b], sp.snap((n + (NF - 1)) // NF * 32))
                            sp.nop().then_inc(S["arrived"], 1)
                            sp.reg_add(c, c, 1)
                        pick(sp, sp.snap(n % NF), 0, NF, arrived)

                def load_ef(j):
                    for b in range(2):
                        if not isinstance(j, int) or j > 0:
                            sp.wait_ge(m1, j * 2 - 1 + b)
                        sp.dma_start(ef[:, b, :], a["ef_t"][:, bass.ds((j * 2 + b) * D, D)]).then_inc(ef_in[b], 16)

                def store_hid(j):
                    for b in range(2):
                        sp.wait_ge(a3, j * 2 + 1 + b)
                        sp.dma_start(hid_d[bass.ds((j * 2 + b) * 4, 4), :, :].rearrange("g p e -> p g e"),
                                     hC[:, b, :].rearrange("p (g e) -> p g e", g=4)).then_inc(hid_out[b], 16)

                if L == 0:
                    peeled(sp, [(0, relay), (0, load_ef), (0, self_rows), (4, store_hid), (3, store_r), (3, store_tab)])
                    sp.wait_ge(S["r_stored"], 16 * NW)
                    sp.wait_ge(S["tab_stored"], 16 * NW)
                else:
                    peeled(sp, [(0, relay), (0, self_rows), (2, load_r0), (5, store_x1), (4, load_x), (7, store_up)])
                    sp.wait_ge(S["x1_stored"], 16 * NW)
                    sp.wait_ge(S["up_stored"], 16 * NW)

            sp.wait_ge(hid_out[0], 16 * (NG // 8))
            sp.wait_ge(hid_out[1], 16 * (NG // 8))
            c = sp.alloc_register("sp_tp_count")
            sp.reg_mov(c, 1)

            def hidden(w):
                lo, hi = window_range(sp, w)
                with sp.Fori(lo, hi) as g:
                    n = sp.snap(c)

                    def load(b):
                        sp.wait_ge(M["w_done"], n)
                        sp.reg_add(c, c, 1)
                        sp.dma_start(hid[:, b, :], hid_d[bass.ds(g, 1), :, :].rearrange("g p e -> p (g e)")).then_inc(
                            M["hid_in"][b], 16)
                    pick(sp, sp.snap(n % 2), 0, 2, load)

            def load_x1(w):
                after(sp, M["out_ready"], w)
                sp.dma_start(xw[:, :], rows(x1_d, w)).then_inc(M["x1_in"], 16)

            def store_out(w):
                sp.wait_ge(M["out_ready"], w + 1)
                if isinstance(w, int) and w == NW - 1:
                    sp.dma_start(out[N - TAIL:N, :], x1[0:TAIL, :]).then_inc(M["stored"], 16)
                else:
                    sp.dma_start(rows(out, w), x1[:, :]).then_inc(M["stored"], 16)

            peeled(sp, [(0, hidden), (2, store_out), (1, load_x1)])
            sp.wait_ge(M["stored"], 16 * NW)

        @block.gpsimd
        def _(g_):
            g_.iota(iota_i[:, :], [[1, P]], base=0, channel_multiplier=0).then_inc(s_cst, 1)
            g_.iota(pid_i[:, :], [[1, 1]], base=0, channel_multiplier=1).then_inc(s_cst, 1)
            g_.iota(asc_i[:, :], [[1, NG]], base=1, channel_multiplier=0).then_inc(s_cst, 1)
            g_.iota(wlo_i[:, :], [[1, 1]], base=0, channel_multiplier=P).then_inc(s_cst, 1)
            g_.memset(eps[:, :], EPS).then_inc(s_cst, 1)
            g_.memset(zeros[:, :], 0.0).then_inc(s_cst, 1)
            g_.memset(w1[:, :], 0.0).then_inc(s_wz, 1)
            g_.memset(w2[:, :], 0.0).then_inc(s_wz, 1)
            g_.memset(w3[:, :], 0.0).then_inc(s_wz, 1)

            def norm_tiles(j, bs):
                for b in bs:
                    g_.wait_ge(n_t, j * 2 + 1 + b)
                    g_.tensor_tensor(tn[:, b, :], tn[:, b, :], bia["g0"][:, :], ALU.mult).then_inc(n_g, 1)
                for b in bs:
                    g_.wait_ge(n_hi, j * 2 + 1 + b)
                    g_.tensor_tensor(tout[:, b, D:], t32[:, b, :], tout[:, b, 0:D], ALU.subtract).then_inc(n_out, 1)

            looped(g_, lambda j: norm_tiles(j, (0, 1)), NW // 2)
            norm_tiles(NW // 2, (0,))

            def gathers(S, table, name, buffers, ring_v, idx_t, idx_by_pool):
                c = g_.alloc_register(f"pool_{name}_count")
                g_.reg_mov(c, 1)
                d = g_.alloc_register(f"pool_{name}_issued")
                g_.reg_mov(d, 0)

                def body(w):
                    lo, hi = window_range(g_, w)
                    with g_.Fori(lo, hi) as g:
                        n = g_.snap(c)
                        if idx_by_pool:
                            g_.wait_ge(S["u_used"], n)
                        else:
                            g_.wait_ge(S["onehot"], n)
                            g_.reg_add(c, c, 1)
                            g_.wait_ge(S["arrived"], n)
                            g_.reg_add(d, d, 1)

                        def gather(b):
                            if idx_by_pool:
                                g_.tensor_copy(idx_t[:, b, :], src_i[:, bass.ds(g * 2, 2)]).then_inc(S["idx_ready"], 1)
                                g_.wait_ge(S["idx_ready"], c)
                                g_.reg_add(c, c, 1)
                            for k in range(2):
                                g_.indirect_dma_start(ring_v[:, b, k, :], None, table,
                                                      bass.IndirectOffsetOnAxis(idx_t[:, b, k:k + 1], 0)).then_inc(S["got"][b % len(S["got"])], 16)
                        pick(g_, g_.snap(n % buffers), 0, buffers, gather)
                peeled(g_, [(0, body)])

            g_.wait_ge(s_edge, 64)
            g_.wait_ge(s_rld, 16)
            g_.wait_ge(t_st[0], 16 * (NW // 2 + 1))
            g_.wait_ge(t_st[1], 16 * (NW // 2))
            gathers(G[0], tab_d[0], "gcn0", NB, ring_h, idx, False)
            g_.wait_ge(G[0]["tab_stored"], 16 * NW)
            gathers(G[1], tab_d[1], "gcn1", NB, ring_h, idx, False)
            g_.wait_ge(G[1]["up_stored"], 16 * NW)
            gathers(M, up_d, "tp", NU, ring_u, idx, True)

        @block.scalar
        def _(ac):
            ac.wait_ge(s_small, 16 * (len(bia) + 4 + 6 + 8))
            ac.mul(w1[:, :], w1[:, :], RB ** -0.5)
            for t in (w2, w3):
                ac.mul(t[:, :], t[:, :], SILU_2MOM * HID ** -0.5)
            ac.mul(w4[:, 0:3 * P], w4[:, 0:3 * P], SILU_2MOM * HID ** -0.5)
            ac.mul(w4[:, 3 * P:], w4[:, 3 * P:], SILU_2MOM * HID ** -0.5 * 3 ** -0.5)
            ac.mul(wup[:, :, :], wup[:, :, :], P ** -0.5)
            ac.mul(wo[:, :, :], wo[:, :, :], (2 * P) ** -0.5 / AVG)
            ac.drain()
            ac.nop().then_inc(s_wsc, 1)
            ac.wait_ge(deg_ready, 1)
            ac.activation(rdeg[:, :], rdeg[:, :], ACT.Sqrt).then_inc(deg_sq, 1)

            def norm_tiles(base, j, bs):
                for b in bs:
                    ac.wait_ge(n_st1, base + 1 + b)
                    ac.activation(mv[:, b, 2:3], mv[:, b, 1:2], ACT.Sqrt, bias=eps[:, 0:1]).then_inc(n_sd1, 1)
                for b in bs:
                    ac.wait_ge(n_rs1, base + 1 + b)
                    ac.activation(hrel[:, b, :], xin[:, b, :], ACT.Relu, bias=mv[:, b, 4:5],
                                  scale=mv[:, b, 3:4]).then_inc(n_h, 1)
                for b in bs:
                    ac.wait_ge(n_st2, base + 1 + b)
                    ac.activation(mv[:, b, 2:3], mv[:, b, 1:2], ACT.Sqrt, bias=eps[:, 0:1]).then_inc(n_sd2, 1)
                for b in bs:
                    ac.wait_ge(n_rs2, base + 1 + b)
                    ac.activation(tn[:, b, :], hrel[:, b, :], ACT.Identity, bias=mv[:, b, 4:5],
                                  scale=mv[:, b, 3:4]).then_inc(n_t, 1)
                for b in bs:
                    ac.wait_ge(n_t32, base + 1 + b)
                    after(ac, t_st[b], j, 16)
                    ac.copy(tout[:, b, 0:D], t32[:, b, :]).then_inc(n_hi, 1)

            looped(ac, lambda j: norm_tiles(j * 2, j, (0, 1)), NW // 2)
            norm_tiles(NW - 1, NW // 2, (0,))
            ac.wait_ge(s_rld, 16)

            for L in range(2):
                S = G[L]

                def self_high(w, S=S, L=L):
                    ac.wait_ge(S["self_in"], (w + 1) * 16)
                    after(ac, S["self_done"], w)
                    ac.mul(hw0[:, :], tw[:, 0:D], col(rse[:, L, :], w)).then_inc(S["self_high"], 1)

                def aggregate(w, S=S, L=L):
                    ac.wait_ge(S["sum_done"], w + 1)
                    after(ac, S["turned"], w)
                    ac.mul(agg[:, :], bank[0][:, :], col(dse[:, L, :], w)).then_inc(S["agg_ready"], 1)

                def copy_at(w, S=S):
                    ac.wait_ge(S["turned"], w + 1)
                    after(ac, S["dense_done"], w)
                    ac.copy(AT[:, 0:4, :], bank[1][:, :].rearrange("p (c n) -> p c n", c=4)).then_inc(S["at_a"], 1)

                def relu_r(w, S=S, L=L):
                    ac.wait_ge(S["y_read"], w + 1)
                    if L == 0:
                        after(ac, S["r_stored"], w, 16)
                    else:
                        after(ac, S["xs_ready"], w)
                    ac.activation(r[:, :], yb[:, :], ACT.Relu).then_inc(S["relu_done"], 1)

                def std(w, S=S):
                    ac.wait_ge(S["stats"], w + 1)
                    ac.activation(mv[:, 0, 2:3], mv[:, 0, 1:2], ACT.Sqrt, bias=eps[:, 0:1]).then_inc(S["std"], 1)

                def scaled(w, S=S):
                    ac.wait_ge(S["scale"], w + 1)
                    ac.activation(tn[:, 0, :], r[:, :], ACT.Identity, bias=mv[:, 0, 4:5],
                                  scale=mv[:, 0, 3:4]).then_inc(S["tn"], 1)

                def high(w, S=S):
                    ac.wait_ge(S["t32"], w + 1)
                    after(ac, S["tab_stored"], w, 16)
                    ac.copy(tout[:, 0, 0:D], t32[:, 0, :]).then_inc(S["high"], 1)

                def copy_xT(w, S=S):
                    ac.wait_ge(S["xs_turned"], w + 1)
                    after(ac, S["proj_done"], w)
                    ac.copy(xT[:, :, :], bank[4][:, :].rearrange("p (c n) -> p c n", c=4)).then_inc(S["xT_ready"], 1)

                def relu_h(w, S=S):
                    ac.wait_ge(S["scale"], w + 1)
                    after(ac, S["h_turned"], w)
                    ac.activation(hrel[:, 0, :], x1[:, :], ACT.Relu, bias=mv[:, 0, 4:5],
                                  scale=mv[:, 0, 3:4]).then_inc(S["h_ready"], 1)

                def copy_hT(w, S=S):
                    ac.wait_ge(S["h_turned"], w + 1)
                    after(ac, S["up_done"], w)
                    ac.copy(hT[:, :, :], bank[6][:, :].rearrange("p (c n) -> p c n", c=4)).then_inc(S["hT_ready"], 1)

                def up_out(w, S=S):
                    ac.wait_ge(S["up_done"], w + 1)
                    after(ac, S["up_stored"], w, 16)
                    ac.copy(uo[:, :], bank[7][:, :]).then_inc(S["up_ready"], 1)

                def act1(j):
                    for b in range(2):
                        ac.wait_ge(m1, j * 2 + 1 + b)
                        if not isinstance(j, int) or j > 0:
                            ac.wait_ge(m2, j * 2 - 1 + b)
                        ac.activation(hA[:, b, :], bank[4 + b][:, :], ACT.Silu).then_inc(a1, 1)

                def act2(j):
                    for b in range(2):
                        ac.wait_ge(m2, j * 2 + 1 + b)
                        if not isinstance(j, int) or j > 0:
                            ac.wait_ge(m3, j * 2 - 1 + b)
                        ac.activation(hB[:, b, :], bank[6 + b][:, :], ACT.Silu).then_inc(a2, 1)

                def act3(j):
                    for b in range(2):
                        after(ac, hid_out[b], j, 16)
                        ac.wait_ge(m3, j * 2 + 1 + b)
                        ac.activation(hC[:, b, :], bank[4 + b][:, :], ACT.Silu).then_inc(a3, 1)

                if L == 0:
                    peeled(ac, [(1, act1), (1, self_high), (2, copy_at), (3, relu_r), (3, std), (3, scaled), (3, high),
                                (0, aggregate), (2, act2), (3, act3), (4, lambda w: None)])
                else:
                    peeled(ac, [(1, self_high), (2, copy_at), (4, copy_xT), (6, copy_hT), (7, up_out), (3, relu_r), (5, std),
                                (5, relu_h), (0, aggregate)])

            c = ac.alloc_register("act_tp_count")
            ac.reg_mov(c, 1)

            for b in range(2):
                ac.wait_ge(hid_out[b], 16 * (NG // 8))
            ac.nop().then_inc(M["w13"], 1)
            ac.nop().then_inc(M["p2"], 1)
            lo_r, hi_r = ac.alloc_register("act_tp_lo"), ac.alloc_register("act_tp_hi")

            def weigh(g):
                n = ac.snap(c)

                def pair(u):
                    b = u % 2
                    ac.wait_ge(M["u_used"], n + (NU - 2))
                    ac.copy(yg[:, b, :], y_t[:, bass.ds(g * 8, 8)])
                    ac.drain()
                    ac.wait_ge(M["got"][u], ac.snap((n + (NU - 1)) // NU * 32))
                    for k in range(2):
                        ins = ac.mul(q0[:, b, k, :], ring_u[:, u, k, P:2 * P], yg[:, b, 4 * k + 1:4 * k + 2])
                    ins.then_inc(M["q0"], 1)
                    ac.wait_ge(M["w_done"], n + 2)
                    ac.wait_ge(M["u_used"], n + (NU - 1))
                    for k in range(2):
                        ins = ac.mul(w13[:, k, :], w_bank[k][0][:, 0:2 * P], yg[:, b, 4 * k:4 * k + 1])
                    ins.then_inc(M["w13"], 1)
                    ac.wait_ge(M["t2"], n)
                    ac.wait_ge(M["seg_done"], n)
                    for k in range(2):
                        for m in range(3):
                            ins = ac.mul(msg[:, b, k, 1, P + m * P:2 * P + m * P], t2[:, k, :],
                                         yg[:, b, 4 * k + 1 + m:4 * k + 2 + m])
                    ins.then_inc(M["p2"], 1)
                    ac.reg_add(c, c, 1)
                pick(ac, ac.snap(n % NU), 0, NU, pair)

            def first_pair(w):
                lo, hi = window_range(ac, w)
                ac.reg_mov(lo_r, lo)
                ac.reg_mov(hi_r, hi)
                weigh(lo)

            def rest(w):
                with ac.Fori(ac.snap(lo_r) + 1, ac.snap(hi_r)) as g:
                    weigh(g)

            def keep_a(w):
                ac.wait_ge(M["sum_done"], w + 1)
                after(ac, M["turned"], w)
                ac.copy(mA[:, :], bank[0][:, :]).then_inc(M["mA"], 1)

            def copy_mT(w):
                ac.wait_ge(M["turned"], w + 1)
                after(ac, M["o_done"], w)
                ac.copy(mT[:, 0:4, :], bank[4][:, :].rearrange("p (c n) -> p c n", c=4)).then_inc(M["mT_a"], 1)

            def window(w):
                rest(w)
                if not isinstance(w, int) or w < NW - 1:
                    first_pair(w + 1)
                keep_a(w)
                copy_mT(w)

            first_pair(0)
            over_windows(ac, window)

        @block.vector
        def _(ve):
            ve.wait_ge(s_edge, 64)
            ve.tensor_scalar(hi_i[:, :], dst_i[:, :], 7, None, ALU.arith_shift_right)
            ve.tensor_scalar(lo_i[:, :], dst_i[:, :], 127, None, ALU.bitwise_and)
            ve.tensor_copy(dst_f[:, :], dst_i[:, :])
            for h in range(2):
                dg = dst_g[:, :].rearrange("p (q e) -> p q e", q=4)
                ve.tensor_reduce(ext[:, h, :], dg, X, ALU.min if h == 0 else ALU.max)
            ve.drain()
            ve.nop().then_inc(s_gext, 1)
            ve.tensor_copy(hi_f[:, :], hi_i[:, :])
            ve.tensor_copy(lo_f[:, :], lo_i[:, :])
            ve.wait_ge(s_cst, 6)
            ve.tensor_copy(iota[:, :], iota_i[:, :])
            ve.tensor_copy(pid[:, :], pid_i[:, :])
            ve.tensor_copy(asc[:, :], asc_i[:, :])
            ve.tensor_copy(wlo[:, :], wlo_i[:, :])
            ve.drain()
            ve.tensor_scalar(ident[:, :], iota[:, :], pid[:, 0:1], None, ALU.is_equal)
            ve.wait_ge(s_small, 16 * (len(bia) + 4 + 6 + 8))
            ve.tensor_tensor(bia["b0"][:, :], bia["b0"][:, :], bia["lb0"][:, :], ALU.add)
            ve.tensor_tensor(bia["b1"][:, :], bia["b1"][:, :], bia["lb1"][:, :], ALU.add)

            ve.wait_ge(s_extld, 16)
            ve.tensor_scalar(rcol[:, 4:5], wlo[:, :], float(P), None, ALU.add)
            ve.tensor_scalar(rtmp[:, :], asc[:, :], -1.0, float(NG + 1), ALU.mult, ALU.add)
            ve.drain()
            ve.scalar_tensor_tensor(out=rtmp2[:, :], in0=extb[:, 1, :], scalar=wlo[:, 0:1], in1=rtmp[:, :],
                                    op0=ALU.is_ge, op1=ALU.mult)
            ve.drain()
            ve.tensor_reduce(rcol[:, 5:6], rtmp2[:, :], X, ALU.max)
            ve.drain()
            ve.tensor_scalar(rcol[:, 6:7], rcol[:, 5:6], -1.0, float(NG), ALU.mult, ALU.add)
            ve.scalar_tensor_tensor(out=rtmp2[:, :], in0=extb[:, 0, :], scalar=rcol[:, 4:5], in1=asc[:, :],
                                    op0=ALU.is_lt, op1=ALU.mult)
            ve.drain()
            ve.tensor_scalar(rcol[:, 0:1], rcol[:, 6:7], float(NG - 2), None, ALU.min)
            ve.tensor_reduce(rcol[:, 5:6], rtmp2[:, :], X, ALU.max)
            ve.drain()
            ve.scalar_tensor_tensor(out=rcol[:, 1:2], in0=rcol[:, 0:1], scalar=2.0, in1=rcol[:, 5:6],
                                    op0=ALU.add, op1=ALU.max)
            ve.drain()
            ve.tensor_copy(rcol_i[:, :], rcol[:, 0:2]).then_inc(s_rcol, 1)

            for L in range(2):
                for i, k in enumerate((f"g{L}", f"be{L}")):
                    ve.tensor_reduce(bound[:, L, i:i + 1], bia[k][:, :], X, ALU.max, apply_absolute_value=True)
                ve.drain()
                ve.scalar_tensor_tensor(out=bound[:, L, 2:3], in0=bound[:, L, 0:1], scalar=22.7, in1=bound[:, L, 1:2],
                                        op0=ALU.mult, op1=ALU.add)
                ve.drain()
                ve.tensor_scalar(bound[:, L, 3:4], bound[:, L, 2:3], 1e-30, None, ALU.max)
                ve.drain()
                ve.tensor_scalar(bound[:, L, 4:5].bitcast(I32), bound[:, L, 3:4].bitcast(I32), 0x7F800000, None,
                                 ALU.bitwise_and)
                ve.drain()
                ve.tensor_scalar(bound[:, L, 5:6], bound[:, L, 4:5], 2.0 ** -14, None, ALU.mult)
                ve.drain()
                ve.reciprocal(bound[:, L, 6:7], bound[:, L, 5:6])
            ve.drain()

            def degree_onehots(j):
                for b in range(2):
                    if not isinstance(j, int):
                        ve.wait_ge(oh_used, j * 2 - 1 + b)
                    at = bass.ds((j * 2 + b) * 8, 8)
                    ve.tensor_tensor(ohl[:, b, :, :], iota[:, :].unsqueeze(1).broadcast_to([P, 8, P]),
                                     lo_f[:, at].unsqueeze(2).broadcast_to([P, 8, P]), ALU.is_equal)
                    ve.tensor_tensor(ohh[:, b, :, :], iota[:, 0:NW].unsqueeze(1).broadcast_to([P, 8, NW]),
                                     hi_f[:, at].unsqueeze(2).broadcast_to([P, 8, NW]), ALU.is_equal).then_inc(oh_rdy, 1)

            looped(ve, degree_onehots, NT // 16)
            ve.wait_ge(deg_sum, 1)
            ve.tensor_scalar(rdeg[:, :], bank[6][:, 0:NW], 1.0, None, ALU.add).then_inc(deg_ready, 1)
            ve.wait_ge(deg_sq, 1)
            ve.reciprocal(dinv[:, :], rdeg[:, :])
            ve.drain()
            ve.tensor_tensor(dinv2[:, :], dinv[:, :], dinv[:, :], ALU.mult)
            for L in range(2):
                ve.tensor_scalar(dup[:, L, :], dinv[:, :], bound[:, L, 6:7], None, ALU.mult)
                ve.tensor_scalar(dse[:, L, :], dinv[:, :], bound[:, L, 5:6], None, ALU.mult)
                ve.tensor_scalar(rse[:, L, :], rdeg[:, :], bound[:, L, 5:6], None, ALU.mult)
            ve.drain()
            ve.nop().then_inc(deg_ready, 1)

            def stats(src, b):
                ve.bn_stats(st[:, b, :], src)
                ve.drain()
                return ve.bn_aggr(mv[:, b, 0:2], st[:, b, :])

            def scale(b, dcol=None):
                ve.reciprocal(mv[:, b, 3:4], mv[:, b, 2:3])
                ve.drain()
                if dcol is not None:
                    ve.tensor_tensor(mv[:, b, 3:4], mv[:, b, 3:4], dcol, ALU.mult)
                    ve.drain()
                return ve.scalar_tensor_tensor(out=mv[:, b, 4:5], in0=mv[:, b, 0:1], scalar=-1.0, in1=mv[:, b, 3:4],
                                               op0=ALU.mult, op1=ALU.mult)

            def affine(b, dst, g, be, dcol):
                ve.tensor_tensor(tn[:, b, :], tn[:, b, :], g[:, :], ALU.mult)
                ve.drain()
                return ve.scalar_tensor_tensor(out=dst, in0=be[:, :], scalar=dcol, in1=tn[:, b, :],
                                               op0=ALU.mult, op1=ALU.add)

            def norm_tiles(base, j, bs):
                for b in bs:
                    ve.wait_ge(x_in[b], (j + 1) * 16)
                    stats(xin[:, b, :], b).then_inc(n_st1, 1)
                for b in bs:
                    ve.wait_ge(n_sd1, base + 1 + b)
                    scale(b).then_inc(n_rs1, 1)
                for b in bs:
                    ve.wait_ge(n_h, base + 1 + b)
                    stats(hrel[:, b, :], b).then_inc(n_st2, 1)
                for b in bs:
                    ve.wait_ge(n_sd2, base + 1 + b)
                    scale(b, col(dup[:, 0, :], base + b)).then_inc(n_rs2, 1)
                for b in bs:
                    ve.wait_ge(n_g, base + 1 + b)
                    if not isinstance(j, int) or j > 0:
                        ve.wait_ge(n_out, base - 1 + b)
                    ve.scalar_tensor_tensor(out=t32[:, b, :], in0=bia["be0"][:, :], scalar=col(dup[:, 0, :], base + b),
                                            in1=tn[:, b, :], op0=ALU.mult, op1=ALU.add).then_inc(n_t32, 1)

            looped(ve, lambda j: norm_tiles(j * 2, j, (0, 1)), NW // 2)
            norm_tiles(NW - 1, NW // 2, (0,))
            ve.wait_ge(s_rld, 16)

            for L in range(2):
                S = G[L]
                c = ve.alloc_register(f"dve_gcn{L}_count")
                ve.reg_mov(c, 1)
                ve.tensor_copy(iota_w[:, :], iota[:, :])

                def onehots(w, S=S, c=c):
                    lo, hi = window_range(ve, w)
                    ve.drain()
                    with ve.Fori(lo, hi) as g:
                        n = ve.snap(c)
                        ve.wait_ge(S["used"], n)
                        ve.tensor_copy(idx[:, bass.ds(n % NB, 1), :].rearrange("p b k -> p (b k)"),
                                       src_i[:, bass.ds(g * 2, 2)])
                        ve.tensor_tensor(ohp[:, bass.ds(n % NB, 1), :, :].rearrange("p b k e -> p (b k) e"),
                                         iota_w[:, :].unsqueeze(1).broadcast_to([P, 2, P]),
                                         dst_f[:, bass.ds(g * 2, 2)].unsqueeze(2).broadcast_to([P, 2, P]),
                                         ALU.is_equal).then_inc(S["onehot"], 1)
                        ve.reg_add(c, c, 1)
                    ve.drain()
                    ve.tensor_scalar(iota_w[:, :], iota_w[:, :], float(P), None, ALU.add)

                def self_rows(w, S=S, L=L):
                    ve.wait_ge(S["self_high"], w + 1)
                    after(ve, S["turned"], w)
                    ve.scalar_tensor_tensor(out=hw[:, :], in0=tw[:, D:], scalar=col(rse[:, L, :], w), in1=hw0[:, :],
                                            op0=ALU.mult, op1=ALU.add)
                    ve.drain()
                    ve.wait_ge(S["agg_ready"], w + 1)
                    ve.scalar_tensor_tensor(out=agg[:, :], in0=hw[:, :], scalar=col(dinv2, w), in1=agg[:, :],
                                            op0=ALU.mult, op1=ALU.add).then_inc(S["self_done"], 1)

                def copy_at(w, S=S):
                    ve.wait_ge(S["turned"], w + 1)
                    after(ve, S["dense_done"], w)
                    ve.tensor_copy(AT[:, 4:8, :], bank[2][:, :].rearrange("p (c n) -> p c n", c=4)).then_inc(S["at_b"], 1)

                def add_bias(w, S=S, L=L):
                    ve.wait_ge(S["dense_done"], w + 1)
                    after(ve, S["relu_done"], w)
                    ve.tensor_tensor(yb[:, :], bank[3][:, :], bia["b0" if L == 0 else "b1"][:, :],
                                     ALU.add).then_inc(S["y_read"], 1)

                def second_norm(w, S=S):
                    ve.wait_ge(S["relu_done"], w + 1)
                    stats(r[:, :], 0).then_inc(S["stats"], 1)
                    ve.wait_ge(S["std"], w + 1)
                    scale(0, col(dup[:, 1, :], w)).then_inc(S["scale"], 1)
                    ve.wait_ge(S["tn"], w + 1)
                    affine(0, t32[:, 0, :], bia["g1"], bia["be1"], col(dup[:, 1, :], w)).then_inc(S["t32"], 1)
                    ve.wait_ge(S["high"], w + 1)
                    ve.tensor_tensor(tout[:, 0, D:], t32[:, 0, :], tout[:, 0, 0:D], ALU.subtract).then_inc(S["tout"], 1)

                def project_in(w, S=S):
                    ve.wait_ge(S["relu_done"], w + 1)
                    ve.wait_ge(S["r0_in"], (w + 1) * 16)
                    after(ve, S["xs_turned"], w)
                    ve.tensor_tensor(xs[:, :], r[:, :], r0w[:, :], ALU.add).then_inc(S["xs_ready"], 1)

                def residual(w, S=S):
                    ve.wait_ge(S["x_in"], (w + 1) * 16)
                    ve.wait_ge(S["proj_done"], w + 1)
                    after(ve, S["x1_stored"], w, 16)
                    after(ve, S["h_ready"], w)
                    ve.tensor_tensor(x1[:, :], bank[5][:, :], bia["pb"][:, :], ALU.add)
                    ve.drain()
                    ve.tensor_tensor(x1[:, :], x1[:, :], xw[:, :], ALU.add).then_inc(S["x1_ready"], 1)
                    ve.drain()
                    stats(x1[:, :], 0).then_inc(S["stats"], 1)
                    ve.wait_ge(S["std"], w + 1)
                    scale(0).then_inc(S["scale"], 1)

                if L == 0:
                    peeled(ve, [(0, onehots), (2, copy_at), (1, self_rows), (3, add_bias), (3, second_norm)])
                else:
                    peeled(ve, [(0, onehots), (2, copy_at), (1, self_rows), (3, add_bias), (3, project_in), (5, residual)])

            c = ve.alloc_register("dve_tp_count")
            ve.reg_mov(c, 1)
            ve.wait_ge(G[1]["x1_stored"], 16 * NW)
            ve.wait_ge(G[1]["up_ready"], NW)
            ve.nop().then_inc(M["u_used"], NU)
            ve.nop().then_inc(M["w_read"], 1)
            ve.tensor_copy(iota_w[:, :], iota[:, :])

            lo_r, hi_r = ve.alloc_register("dve_tp_lo"), ve.alloc_register("dve_tp_hi")

            def messages(g):
                n = ve.snap(c)

                def pair(ub):
                    b, u = ub % 2, ring_u[:, ub, :, :]
                    ve.wait_ge(M["q0"], n)
                    for k in range(2):
                        ve.scalar_tensor_tensor(out=q1[:, k, :], in0=u[:, k, 2 * P:3 * P],
                                                scalar=yg[:, b, 4 * k + 2:4 * k + 3],
                                                in1=q0[:, b, k, :], op0=ALU.mult, op1=ALU.add)
                    ve.wait_ge(M["seg_done"], n)
                    ve.tensor_tensor(oh[:, b, :, :], iota_w[:, :].unsqueeze(1).broadcast_to([P, 2, P]),
                                     dst_f[:, bass.ds(g * 2, 2)].unsqueeze(2).broadcast_to([P, 2, P]), ALU.is_equal)
                    ve.drain()
                    for k in range(2):
                        ve.scalar_tensor_tensor(out=q2[:, k, :], in0=u[:, k, 3 * P:4 * P],
                                                scalar=yg[:, b, 4 * k + 3:4 * k + 4],
                                                in1=q1[:, k, :], op0=ALU.mult, op1=ALU.add)
                    ve.wait_ge(M["w_done"], n + 2)
                    ve.wait_ge(M["p2"], n)
                    for k in range(2):
                        ins = ve.tensor_tensor(t2[:, k, :], w_bank[k][1][:, 0:P], u[:, k, 0:P], ALU.mult)
                    ins.then_inc(M["t2"], 1)
                    ve.drain()
                    for k in range(2):
                        ins = ve.tensor_tensor(msg[:, b, k, 1, 0:P], q2[:, k, :], w_bank[k][1][:, P:2 * P], ALU.mult)
                    ins.then_inc(M["w_read"], 1)
                    ve.wait_ge(M["w13"], n + 1)
                    for k in range(2):
                        ve.tensor_tensor(msg[:, b, k, 0, 0:P], w13[:, k, 0:P], u[:, k, 0:P], ALU.mult)
                        ins = ve.tensor_tensor(msg[:, b, k, 0, P:].rearrange("p (m u) -> p m u", m=3),
                                               w13[:, k, P:2 * P].unsqueeze(1).broadcast_to([P, 3, P]),
                                               u[:, k, P:4 * P].rearrange("p (m u) -> p m u", m=3), ALU.mult)
                    ins.then_inc(M["u_used"], 1)
                    ve.reg_add(c, c, 1)
                pick(ve, ve.snap(n % NU), 0, NU, pair)

            def first_pair(w):
                lo, hi = window_range(ve, w)
                ve.reg_mov(lo_r, lo)
                ve.reg_mov(hi_r, hi)
                messages(lo)

            def rest(w):
                with ve.Fori(ve.snap(lo_r) + 1, ve.snap(hi_r)) as g:
                    messages(g)
                ve.drain()
                ve.tensor_scalar(iota_w[:, :], iota_w[:, :], float(P), None, ALU.add)
                ve.drain()

            def keep_b(w):
                ve.wait_ge(M["sum_done"], w + 1)
                after(ve, M["turned"], w)
                ve.tensor_copy(mB[:, :], bank[1][:, :]).then_inc(M["mB"], 1)

            def copy_mT(w):
                ve.wait_ge(M["turned"], w + 1)
                after(ve, M["o_done"], w)
                ve.tensor_copy(mT[:, 4:8, :], m_bank[1][:, :].rearrange("p (c n) -> p c n", c=4)).then_inc(M["mT_b"], 1)

            def finish(w):
                ve.wait_ge(M["x1_in"], (w + 1) * 16)
                ve.wait_ge(M["o_done"], w + 1)
                after(ve, M["stored"], w, 16)
                ve.tensor_tensor(x1[:, 0:P], xw[:, 0:P], bank[6][:, 0:P], ALU.add)
                ve.tensor_tensor(x1[:, P:].rearrange("p (v m) -> p v m", m=3), xw[:, P:].rearrange("p (v m) -> p v m", m=3),
                                 bank[6][:, P:].rearrange("p (m v) -> p v m", m=3), ALU.add).then_inc(M["out_ready"], 1)

            def window(w):
                rest(w)
                if not isinstance(w, int) or w > 0:
                    finish(w - 1)
                if not isinstance(w, int) or w < NW - 1:
                    first_pair(w + 1)
                keep_b(w)
                copy_mT(w)

            ve.drain()
            first_pair(0)
            over_windows(ve, window)
            finish(NW - 1)

        @block.tensor
        def _(pe):
            pe.wait_ge(s_wsc, 1)

            def touch(t, n, start):
                return pe.matmul(t, zeros[:, 0:P], zeros[:, 0:n], start=start, stop=not start, skip_group_check=True)

            def degrees(j, b):
                pe.wait_ge(oh_rdy, j * 2 + 1 + b)
                for t in range(8):
                    ins = pe.matmul(bank[6][:, 0:NW], ohl[:, b, t, :], ohh[:, b, t, :], start=False, stop=False,
                                    skip_group_check=True)
                ins.then_inc(oh_used, 1)

            def histogram(j):
                degrees(j, 0)
                degrees(j, 1)

            touch(bank[6][:, 0:NW], NW, True)
            looped(pe, histogram, NT // 16)
            touch(bank[6][:, 0:NW], NW, False).then_inc(deg_sum, 1)
            pe.wait_ge(s_big, 16 * len(W))
            pe.wait_ge(deg_ready, 1)
            pe.wait_ge(s_rld, 16)

            for L in range(2):
                S = G[L]
                WC, WL = (W["W0"], W["lw0"]) if L == 0 else (W["W1"], W["lw1"])
                c = pe.alloc_register(f"pe_gcn{L}_count")
                pe.reg_mov(c, 1)
                pe.nop().then_inc(S["used"], NB)
                pe.nop().then_inc(S["arrived"], NF)

                def edge_sum(w, S=S, c=c):
                    lo, hi = window_range(pe, w)
                    after(pe, S["agg_ready"], w)
                    touch(bank[0][:, :], D, True)
                    with pe.Fori(lo, hi) as g:
                        n = pe.snap(c)
                        pe.wait_ge(S["arrived"], n + NF)
                        at = pe.snap(n % NB * 2)
                        for k in range(2):
                            for h in range(2):
                                ins = pe.matmul(bank[0][:, :], ohp_k[:, bass.ds(at + k, 1), :].rearrange("p b n -> p (b n)"),
                                                ring_k[:, bass.ds((at + k) * 2 + h, 1), :].rearrange("p b n -> p (b n)"),
                                                start=False, stop=False, skip_group_check=True)
                        ins.then_inc(S["used"], 1)
                        pe.reg_add(c, c, 1)
                    touch(bank[0][:, :], D, False).then_inc(S["sum_done"], 1)

                def turn(w, S=S):
                    pe.wait_ge(S["self_done"], w + 1)
                    after(pe, S["at_a"], w)
                    after(pe, S["at_b"], w)
                    for i in range(8):
                        sr = (agg if i < 4 else hw)[:, (i % 4) * P:(i % 4 + 1) * P]
                        ins = pe.transpose(bank[1 + i // 4][:, (i % 4) * P:(i % 4 + 1) * P], sr, ident[:, :])
                    ins.then_inc(S["turned"], 1)

                def dense(w, S=S, WC=WC, WL=WL):
                    pe.wait_ge(S["at_a"], w + 1)
                    pe.wait_ge(S["at_b"], w + 1)
                    after(pe, S["y_read"], w)
                    for i in range(8):
                        ins = pe.matmul(bank[3][:, :], AT[:, i, :], (WC if i < 4 else WL)[:, i % 4, :],
                                        start=(i == 0), stop=(i == 7))
                    ins.then_inc(S["dense_done"], 1)

                def turn_xs(w, S=S):
                    pe.wait_ge(S["xs_ready"], w + 1)
                    after(pe, S["xT_ready"], w)
                    for i in range(4):
                        ins = pe.transpose(bank[4][:, i * P:(i + 1) * P], xs[:, i * P:(i + 1) * P], ident[:, :])
                    ins.then_inc(S["xs_turned"], 1)

                def project(w, S=S):
                    pe.wait_ge(S["xT_ready"], w + 1)
                    after(pe, S["x1_ready"], w)
                    for i in range(4):
                        ins = pe.matmul(bank[5][:, :], xT[:, i, :], W["pw"][:, i, :], start=(i == 0), stop=(i == 3))
                    ins.then_inc(S["proj_done"], 1)

                def turn_h(w, S=S):
                    pe.wait_ge(S["h_ready"], w + 1)
                    after(pe, S["hT_ready"], w)
                    for i in range(4):
                        sr = hrel[:, 0, 0:P] if i == 0 else hrel[:, 0, P:].rearrange("p (u m) -> p m u", m=3)[:, i - 1, :]
                        ins = pe.transpose(bank[6][:, i * P:(i + 1) * P], sr, ident[:, :])
                    ins.then_inc(S["h_turned"], 1)

                def up(w, S=S):
                    pe.wait_ge(S["hT_ready"], w + 1)
                    after(pe, S["up_ready"], w)
                    for i in range(4):
                        ins = pe.matmul(bank[7][:, i * P:(i + 1) * P], hT[:, i, :], wup[:, min(i, 1), :], start=True, stop=True)
                    ins.then_inc(S["up_done"], 1)

                def layer1(j):
                    for b in range(2):
                        pe.wait_ge(ef_in[b], j * 16 + 16)
                        if not isinstance(j, int) or j > 2:
                            pe.wait_ge(a3, j * 2 - 5 + b)
                        elif j > 0:
                            pe.wait_ge(a1, j * 2 - 1 + b)
                        pe.matmul(bank[4 + b][:, :], w1[:, :], ef[:, b, :], start=True, stop=True).then_inc(m1, 1)

                def layer2(j):
                    for b in range(2):
                        pe.wait_ge(a1, j * 2 + 1 + b)
                        if not isinstance(j, int) or j > 0:
                            pe.wait_ge(a2, j * 2 - 1 + b)
                        pe.matmul(bank[6 + b][:, :], w2[:, :], hA[:, b, :], start=True, stop=True).then_inc(m2, 1)

                def layer3(j):
                    for b in range(2):
                        pe.wait_ge(a2, j * 2 + 1 + b)
                        if not isinstance(j, int) or j > 0:
                            pe.wait_ge(a3, j * 2 - 1 + b)
                        if isinstance(j, int):
                            pe.wait_ge(a1, min(2 * j + 6, NG // 4))
                        else:
                            pe.wait_ge(a1, j * 2 + 6)
                        pe.matmul(bank[4 + b][:, :], w3[:, :], hB[:, b, :], start=True, stop=True).then_inc(m3, 1)

                if L == 0:
                    peeled(pe, [(2, layer2), (0, edge_sum), (1, turn), (3, layer3), (2, dense), (0, layer1),
                                (4, lambda w: None)])
                    pe.wait_ge(a3, NG // 4)
                else:
                    peeled(pe, [(0, edge_sum), (1, turn), (2, dense), (3, turn_xs), (4, project), (5, turn_h), (6, up)])

            c = pe.alloc_register("pe_tp_count")
            pe.reg_mov(c, 1)
            pe.wait_ge(G[1]["up_ready"], NW)
            pe.wait_ge(G[1]["agg_ready"], NW)
            pe.wait_ge(G[1]["x1_ready"], NW)
            pe.nop().then_inc(M["w_done"], 2)
            pe.nop().then_inc(M["seg_done"], 2)

            def edge_weights(n, b):
                pe.wait_ge(M["hid_in"][b], 16 if isinstance(n, int) else pe.snap((n + 1) // 2 * 16))
                pe.wait_ge(M["w_read"], n)
                pe.wait_ge(M["w13"], n)
                for h in range(2):
                    for k in range(2):
                        ins = pe.matmul(w_bank[k][h][:, 0:2 * P], hid[k * HID:(k + 1) * HID, b, :],
                                        w4[k * HID:(k + 1) * HID, h * 2 * P:(h + 1) * 2 * P], start=True, stop=True)
                ins.then_inc(M["w_done"], 1)

            def sum_pair(n, b):
                pe.wait_ge(M["u_used"], n + NU)
                pe.wait_ge(M["p2"], n + 1)
                for k in range(2):
                    for h in range(2):
                        ins = pe.matmul(bank[h][:, :], oh[:, b, k, :], msg[:, b, k, h, :], start=False, stop=False,
                                        skip_group_check=True)
                ins.then_inc(M["seg_done"], 1)

            def turn_m(w):
                pe.wait_ge(M["mA"], w + 1)
                pe.wait_ge(M["mB"], w + 1)
                after(pe, M["mT_a"], w)
                after(pe, M["mT_b"], w)
                after(pe, M["out_ready"], w)
                for i in range(8):
                    sr = (mA if i < 4 else mB)[:, (i % 4) * P:(i % 4 + 1) * P]
                    ins = pe.transpose(m_bank[i // 4][:, (i % 4) * P:(i % 4 + 1) * P], sr, ident[:, :])
                ins.then_inc(M["turned"], 1)

            def out_product(w):
                pe.wait_ge(M["mT_a"], w + 1)
                pe.wait_ge(M["mT_b"], w + 1)
                after(pe, M["out_ready"], w)
                for i in range(4):
                    first, second = (0, 4) if i == 0 else (4 + i, i)
                    o = bank[6][:, i * P:(i + 1) * P]
                    pe.matmul(o, mT[:, first, :], wo[:, 0 if i == 0 else 2, :], start=True, stop=False)
                    ins = pe.matmul(o, mT[:, second, :], wo[:, 1 if i == 0 else 3, :], start=False, stop=True)
                ins.then_inc(M["o_done"], 1)

            def weights_ahead():
                n = pe.snap(c)

                def step(b):
                    edge_weights(n, b)
                    sum_pair(n - 1, 1 - b)
                pick(pe, pe.snap(n % 2), 0, 2, step)
                pe.reg_add(c, c, 1)

            def window(w):
                lo, hi = window_range(pe, w)
                after(pe, M["mA"], w)
                after(pe, M["mB"], w)
                touch(bank[0][:, :], D, True)
                touch(bank[1][:, :], D, True)
                if not isinstance(w, int) or w > 0:
                    turn_m(w - 1)
                with pe.Fori(lo + 1, hi) as g:
                    weights_ahead()
                if not isinstance(w, int) or w > 0:
                    out_product(w - 1)
                if not isinstance(w, int) or w < NW - 1:
                    weights_ahead()
                else:
                    n = pe.snap(c)
                    pick(pe, pe.snap(n % 2), 0, 2, lambda b: sum_pair(n - 1, 1 - b))
                touch(bank[0][:, :], D, False)
                touch(bank[1][:, :], D, False).then_inc(M["sum_done"], 1)

            edge_weights(1, 1)
            pe.reg_add(c, c, 1)
            over_windows(pe, window)
            turn_m(NW - 1)
            out_product(NW - 1)


_SHORT = {"W0": "L0_gnn_W0", "b0": "L0_gnn_b0", "lb0": "L0_gnn_lb0", "g0": "L0_gnn_g0", "be0": "L0_gnn_be0",
          "W1": "L0_gnn_W1", "b1": "L0_gnn_b1", "lb1": "L0_gnn_lb1", "g1": "L0_gnn_g1", "be1": "L0_gnn_be1",
          "pb": "L0_gnn_pb", "W_up0": "L1_gnn_W_up0", "W_up1": "L1_gnn_W_up1", "W_mlp1": "L1_gnn_W_mlp1",
          "W_mlp2": "L1_gnn_W_mlp2", "W_mlp3": "L1_gnn_W_mlp3", "W_mlp4": "L1_gnn_W_mlp4",
          "W_out0": "L1_gnn_W_out0", "W_out1": "L1_gnn_W_out1", "x": "x"}


def kernel(**inputs):
    import numpy as _np
    import concourse.bacc as _bacc
    from concourse import mybir as _mybir
    from concourse.bass_utils import run_bass_kernel_spmd as _run

    nc = _bacc.Bacc("TRN2", target_bir_lowering=False, num_devices=1)
    laid = {k: _np.asarray(inputs[v]) for k, v in _SHORT.items()}
    for k, v in (("lw0", "L0_gnn_lw0"), ("lw1", "L0_gnn_lw1"), ("pw", "L0_gnn_pw")):
        laid[k] = _np.asarray(inputs[v]).T
    pad = NT * P - E
    src, dst = _np.asarray(inputs["src"]), _np.asarray(inputs["dst"])
    ea, ef = _np.asarray(inputs["edge_attr_4"]), _np.asarray(inputs["edge_attr_8"])
    laid["src_t"] = _np.pad(src, (0, pad)).reshape(NT, P).T
    laid["dst_t"] = _np.pad(dst, (0, pad), constant_values=-1).reshape(NT, P).T
    laid["dst_g"] = _np.pad(dst, (0, pad), mode="edge").reshape(NG // 4, 4 * 256)
    laid["ea_t"] = _np.pad(ea, ((0, pad), (0, 0))).reshape(NT, P, 4).transpose(1, 0, 2).reshape(P, NT * 4)
    laid["ef_t"] = (_np.pad(ef, ((0, pad), (0, 0))).reshape(NG, 2, P, RB).transpose(1, 3, 0, 2)
                    .reshape(2 * RB, NG * P))
    arrays, args = {}, {}
    for name, v in laid.items():
        v = _np.ascontiguousarray(v)
        arrays[f"in_{name}_dram"] = v
        args[name] = nc.dram_tensor(f"in_{name}_dram", v.shape, _mybir.dt.from_np(v.dtype), kind="ExternalInput").ap()
    out = nc.dram_tensor("out_0_dram", (N, D), _mybir.dt.float32, kind="ExternalOutput").ap()
    build(nc, args, out)
    r = _run(nc, [arrays], core_ids=[0])
    return r.results[0]["out_0_dram"]
```
